# Optimizing a Trainium2 kernel written in Bass

```python
import numpy as np
import jax
import jax.numpy as jnp

def _softmax(x, axis=-1):
    return jax.nn.softmax(x, axis=axis)

def _gelu(x):
    return jax.nn.gelu(x, approximate=True)

def _silu(x):
    return jax.nn.silu(x)

def _sigmoid(x):
    return jax.nn.sigmoid(x)

def _layernorm(x, axis=-1, eps=1e-05):
    m = jnp.mean(x, axis=axis, keepdims=True)
    v = jnp.var(x, axis=axis, keepdims=True)
    return (x - m) / jnp.sqrt(v + eps)

def _scatter_add(tgt, idx, src, axis=0):
    return tgt.at[idx].add(src)

def _segment_sum(src, seg, n):
    return jax.ops.segment_sum(src, seg, n)
kernel_name = 'mk_gnn_resnorm_d2_gnn_r8_7d9b43'

def setup_inputs(seed: int=0):
    np.random.seed(seed)
    _w = jnp.asarray

    def _rec_inputs():
        import jax
        import jax.numpy as jnp
        _gk = jax.random.key(seed)
        x = 0.0001712 + 1 * jax.random.normal(jax.random.fold_in(_gk, 1), (12500, 16), jnp.float32)
        src = jax.random.randint(jax.random.fold_in(_gk, 2), (400000,), 0, 12500, jnp.int32)
        dst = jax.random.randint(jax.random.fold_in(_gk, 3), (400000,), 0, 12500, jnp.int32)
        _o = jnp.argsort(dst, stable=True)
        src = src[_o]
        dst = dst[_o]
        return (x, src, dst)
    x, src, dst = _rec_inputs()

    def _L0_gnn_setup():
        import jax, jax.numpy as jnp
        import numpy as np
        STALK_DIM = 16
        N_NODES = 6250
        N_EDGES = 50000
        HIDDEN = 64
        key = jax.random.key(seed)
        k1, k2, k3, k4 = jax.random.split(key, 4)
        d = STALK_DIM
        x = jax.random.normal(k1, (N_NODES, d), dtype=jnp.float32)
        edge_index = jax.random.randint(k2, (2, N_EDGES), 0, N_NODES, dtype=jnp.int64)
        W1 = jax.random.normal(k3, (HIDDEN, 2 * d), dtype=jnp.float32) * (1.0 / np.sqrt(2 * d))
        b1 = jnp.zeros((HIDDEN,), dtype=jnp.float32)
        W2 = jax.random.normal(k4, (d, HIDDEN), dtype=jnp.float32) * (1.0 / np.sqrt(HIDDEN))
        b2 = jnp.zeros((d,), dtype=jnp.float32)
        return {'x': x, 'edge_index': edge_index, 'W1': W1, 'b1': b1, 'W2': W2, 'b2': b2}
    _L0_gnn_all = _L0_gnn_setup()
    _L0_gnn_in = {k: v for k, v in _L0_gnn_all.items() if k in ('W1', 'b1', 'W2', 'b2')}
    del _L0_gnn_all

    def _L1_gnn_setup():
        import jax, jax.numpy as jnp
        import numpy as np
        key = jax.random.key(seed)
        k1, k2, k3, k4 = jax.random.split(key, 4)
        N, E, D = (12500, 400000, 16)
        x = jax.random.normal(k1, (N, D), dtype=jnp.float32)
        edge_index = jax.random.randint(k2, (2, E), 0, N, dtype=jnp.int64)
        s = 1.0 / np.sqrt(D)
        W1 = jax.random.normal(k3, (D, 16), dtype=jnp.float32) * s
        b1 = jnp.zeros((16,), dtype=jnp.float32)
        W2 = jax.random.normal(k4, (16, 16), dtype=jnp.float32) * s
        b2 = jnp.zeros((16,), dtype=jnp.float32)
        return {'x': x, 'edge_index': edge_index, 'W1': W1, 'b1': b1, 'W2': W2, 'b2': b2}
    _L1_gnn_all = _L1_gnn_setup()
    _L1_gnn_in = {k: v for k, v in _L1_gnn_all.items() if k in ('W1', 'b1', 'W2', 'b2')}
    del _L1_gnn_all
    return {'x': x, 'src': src, 'dst': dst, 'L0_gnn_W1': _L0_gnn_in['W1'], 'L0_gnn_b1': _L0_gnn_in['b1'], 'L0_gnn_W2': _L0_gnn_in['W2'], 'L0_gnn_b2': _L0_gnn_in['b2'], 'L1_gnn_W1': _L1_gnn_in['W1'], 'L1_gnn_b1': _L1_gnn_in['b1'], 'L1_gnn_W2': _L1_gnn_in['W2'], 'L1_gnn_b2': _L1_gnn_in['b2']}

def reference(x, src, dst, L0_gnn_W1, L0_gnn_b1, L0_gnn_W2, L0_gnn_b2, L1_gnn_W1, L1_gnn_b1, L1_gnn_W2, L1_gnn_b2):
    import jax
    import jax.numpy as jnp

    def _L0_gnn_ref(x, edge_index, W1, b1, W2, b2):
        import jax, jax.numpy as jnp
        import numpy as np
        STALK_DIM = 16
        N_NODES = 6250
        N_EDGES = 50000
        HIDDEN = 64
        d = x.shape[1]
        n = x.shape[0]
        src, dst = (edge_index[0], edge_index[1])
        xs, xd = (x[src], x[dst])

        def reflection(a, b):
            h = jax.nn.relu(jnp.concatenate([a, b], axis=1) @ W1.T + b1)
            return h @ W2.T + b2

        def householder(v):
            vn = v / jnp.maximum(jnp.linalg.norm(v, axis=1, keepdims=True), 1e-12)
            return jnp.eye(d, dtype=v.dtype)[None] - 2.0 * vn[:, :, None] * vn[:, None, :]
        F_s = householder(reflection(xs, xd))
        F_d = householder(reflection(xd, xs))
        L_sd = -jnp.einsum('eki,ekj->eij', F_s, F_d)
        ones_e = jnp.ones(src.shape[0], dtype=x.dtype)
        deg = jnp.zeros(n, dtype=x.dtype).at[src].add(ones_e).at[dst].add(ones_e)
        deg_inv_sqrt = 1.0 / jnp.sqrt(jnp.maximum(deg, 1e-05))
        coef = deg_inv_sqrt[src] * deg_inv_sqrt[dst]
        msg_s = coef[:, None] * jnp.einsum('eij,ej->ei', L_sd, xd)
        msg_d = coef[:, None] * jnp.einsum('eji,ej->ei', L_sd, xs)
        out = x - jnp.zeros_like(x).at[src].add(msg_s) - jnp.zeros_like(x).at[dst].add(msg_d)
        return jax.nn.relu(out)

    def _L1_gnn_ref(x, edge_index, W1, b1, W2, b2):
        import jax, jax.numpy as jnp
        import numpy as np
        N = x.shape[0]
        loop = jnp.arange(N, dtype=edge_index.dtype)
        row = jnp.concatenate([edge_index[0], loop])
        col = jnp.concatenate([edge_index[1], loop])
        deg = jax.ops.segment_sum(jnp.ones_like(col, dtype=x.dtype), col, num_segments=N)
        dinv = jnp.where(deg > 0, jax.lax.rsqrt(deg), 0.0)
        norm = dinv[row] * dinv[col]

        def gcn_conv(h, W, b):
            hw = h @ W
            msg = hw[row] * norm[:, None]
            agg = jax.ops.segment_sum(msg, col, num_segments=N)
            return agg + b
        h = jnp.tanh(gcn_conv(x, W1, b1))
        h = jnp.tanh(gcn_conv(h, W2, b2))
        return h
    edge_index = jnp.stack([src, dst])
    x = _layernorm(x + _L0_gnn_ref(x, edge_index, L0_gnn_W1, L0_gnn_b1, L0_gnn_W2, L0_gnn_b2), axis=-1)
    x = _layernorm(x + _L1_gnn_ref(x, edge_index, L1_gnn_W1, L1_gnn_b1, L1_gnn_W2, L1_gnn_b2), axis=-1)
    return x

_drawn_inputs = setup_inputs


def setup_inputs(seed=0):
    import zlib

    import numpy as np

    out = dict(_drawn_inputs(seed))
    spreads = {'L0_gnn_b1': (0.0, 0.8),
     'L0_gnn_b2': (0.0, 0.53),
     'L1_gnn_b1': (0.0, 0.1),
     'L1_gnn_b2': (0.0, 0.1)}
    factors = {}
    for name, (base, spread) in spreads.items():
        noise = np.random.default_rng([zlib.crc32(name.encode()), seed]).standard_normal(out[name].shape)
        drawn = base * np.exp(spread * noise) if base else spread * noise
        out[name] = jnp.asarray(drawn.astype(out[name].dtype))
    for name, factor in factors.items():
        out[name] = (out[name] * factor).astype(out[name].dtype)
    return out
```

```python
import numpy as np
import concourse.bass as bass
import concourse.mybir as mybir
from contextlib import ExitStack


def ceil_div(a, b):
    return -(-a // b)


def gnn_kernel(nc, x, src, dst, mlp_w1, mlp_b1, mlp_w2, mlp_b2, gcn_w1, gcn_b1, gcn_w2, gcn_b2, out):
    F32, I32, BF16 = mybir.dt.float32, mybir.dt.int32, mybir.dt.bfloat16
    ALU, ACT, AX = mybir.AluOpType, mybir.ActivationFunctionType, mybir.AxisListType

    P = 128
    N, D = x.shape
    E = src.shape[0]
    HID = mlp_w1.shape[0]
    EP = E // P
    T = 25
    SLOTS = 5
    ITERS = EP // (T * SLOTS)
    STEP = T * SLOTS
    BATCH = 5
    BATCHES = T // BATCH
    BANK = 512
    SUBS = ceil_div(T, BANK // P)
    PARTS = [range(j * T // SUBS, (j + 1) * T // SUBS) for j in range(SUBS)]
    assert all(len(c) * P <= BANK for c in PARTS)
    assert EP * P == E and ITERS * STEP == EP and 2 * HID == P and 2 * D == 32
    NB = ceil_div(N, P)
    PER = P // D
    NG = ceil_div(NB, PER)
    NBP = NG * PER
    NPAD = NB * P
    TAIL = N - (NB - 1) * P
    R = D + 1
    COPIES = BATCH
    SKIP = 1 << 14
    FAR = 1 << 20
    assert SKIP >= NPAD and FAR >= E
    LN_EPS, DEG_MIN, NORM_MIN = 1e-5, 1e-5, 1e-24

    ctx = ExitStack()
    with ctx:
        ctx.enter_context(nc.allow_non_contiguous_dma(reason="small transposed weights"))

        def sb(name, shape, dt=F32):
            return ctx.enter_context(nc.sbuf_tensor(name, shape, dt))

        def sem(name):
            return ctx.enter_context(nc.semaphore(name))

        def sems(name):
            return [sem(f"{name}{k}") for k in range(SLOTS)]

        def dram(name, shape):
            return nc.dram_tensor(name, shape, F32, kind="Internal").ap()

        table0 = dram("table0", [NPAD, R])
        tables = [dram(f"table{l}", [NPAD, D]) for l in (1, 2)]
        xd_rows = dram("xd_rows", [E, R])
        runsums = [dram(f"runsum{l}", [E, D]) for l in range(3)]
        src_sums = [dram(f"src_sum{c}", [NPAD, D]) for c in range(COPIES)]

        src_i = sb("src_i", [P, EP + STEP], I32)
        keep = sb("keep", [P, EP + STEP])
        prev_last = sb("prev_last", [P, 1], I32)
        next_first = sb("next_first", [P, 1], I32)
        first_i = sb("first_i", [P, 1], I32)
        last_lohi_i = sb("last_lohi_i", [P, 2], I32)
        last_lohi = sb("last_lohi", [P, 2])
        runs_on = sb("runs_on", [P, 1])
        iota_lo = sb("iota_lo", [P, P, T], BF16)
        iota_f = sb("iota_f", [P, P])
        ident = sb("ident", [P, P])
        before = sb("before", [P, P])
        ones = sb("ones", [P, P])
        pow_i = sb("pow_i", [P, 1], I32)
        pow2_i = sb("pow2_i", [P, 1], I32)
        pow2 = pow2_i[:, :].bitcast(F32)
        lead_max = sb("lead_max", [P, 1])
        zeros = sb("zeros", [P, STEP * R])
        w1c = sb("w1c", [2 * D, P])
        b1c = sb("b1c", [P, 1])
        w2c = sb("w2c", [P, 2 * D])
        b2c = sb("b2c", [P, 2 * D])
        gcn_w = [sb(f"gcn_w{l}", [P, P]) for l in (1, 2)]
        gcn_b = [sb(f"gcn_b{l}", [P, D]) for l in (1, 2)]

        WORDS = 2 * EP + T * P + T * NB + 64
        shared = sb("shared", [P, WORDS])
        half = shared[:, :].bitcast(BF16)
        lohi = [[half[:, (2 * e + h) * EP:(2 * e + h + 1) * EP] for h in range(2)] for e in range(2)]
        hot_at = 4 * EP
        hot_lo = [half[:, hot_at + e * P * T:hot_at + (e + 1) * P * T].rearrange("p (j t) -> p j t", t=T)
                  for e in range(2)]
        hot_at += 2 * P * T
        hot_hi = [half[:, hot_at + e * NB * T:hot_at + (e + 1) * NB * T].rearrange("p (j t) -> p j t", t=T)
                  for e in range(2)]
        split_i = shared[:, 2 * EP:3 * EP].bitcast(I32)
        same = shared[:, 0:T * P].rearrange("p (t e) -> p t e", e=P)
        at = T * P
        pairs = []
        for _ in range(5):
            pairs.append(shared[:, at:at + T * 2 * D].rearrange("p (t s c) -> p t s c", t=T, s=2))
            at += T * 2 * D
        refl, xw, prod, mirrored, msgs = pairs
        dots = shared[:, at:at + 2 * T].rearrange("p (t s) -> p t s", s=2)
        scale2 = shared[:, at + 2 * T:at + 4 * T].rearrange("p (t s) -> p t s", s=2)
        late = shared[:, at + 4 * T:at + 5 * T]
        assert at + 5 * T <= WORDS
        acc_in = [shared[:, c * NB * D:(c + 1) * NB * D].rearrange("p (h c) -> p h c", c=D)
                  for c in range(COPIES)]
        assert COPIES * NB * D <= WORDS

        shared2 = sb("shared2", [P, 2 * SLOTS * T * D])
        dst_i = shared2[:, 0:EP].bitcast(I32)
        sums = shared2[:, 0:SLOTS * T * D].rearrange("p (k t c) -> p k t c", k=SLOTS, t=T)
        merged = shared2[:, SLOTS * T * D:].rearrange("p (k t c) -> p k t c", k=SLOTS, t=T)

        idx = sb("idx", [P, SLOTS, T], I32)
        src_f = sb("src_f", [P, SLOTS, T])
        keep_s = sb("keep_s", [P, SLOTS, T])
        put_i = sb("put_i", [P, SLOTS, T], I32)
        xsd = sb("xsd", [P, SLOTS, T, 2 * R])
        first_tab = sb("first_tab", [P, R])
        xd_in = sb("xd_in", [P, SLOTS, T, R])
        rows = xd_in[:, :, :, 0:D]
        rows = xd_in[:, :, :, :].rearrange("p k t c -> p (k t c)")[:, 0:SLOTS * T * D].rearrange(
            "p (k t c) -> p k t c", k=SLOTS, t=T)
        xt = sb("xt", [2 * D, BANK])
        hid = sb("hid", [P, BANK])

        node_x = sb("node_x", [P, NBP, D])
        node_tab = sb("node_tab", [P, NB, R + 1])
        agg = sb("agg", [P, NB, D])
        tmp = sb("tmp", [P, NB, D])
        node_h = sb("node_h", [P, NBP, D])
        node_t = sb("node_t", [P, NB, D])
        node_xt = sb("node_xt", [P, NG * P])
        cnt = sb("cnt", [P, 2, NB])
        start = sb("start", [P, NB])
        total = sb("total", [P, NB])
        start_i = sb("start_i", [P, NB], I32)
        end_i = sb("end_i", [P, NB], I32)
        has_in = sb("has_in", [P, NB])
        dinv = sb("dinv", [P, NB])
        dis = sb("dis", [P, NB])
        st = [sb(f"st{i}", [P, NB]) for i in range(4)]
        last_hi = sb("last_hi", [P, NB])
        last_lo = sb("last_lo", [P, P])
        last_row = sb("last_row", [P, D])

        ps = ctx.enter_context(nc.psum_tensor("ps", [P, 8 * BANK], F32))
        ps_xt = ps[0:2 * D, 0:BANK]
        ps_eq = ps[:, BANK:2 * BANK].rearrange("p (t e) -> p t e", e=P)
        ps_h = ps[:, 2 * BANK:3 * BANK]
        ps_ld = ps[:, 3 * BANK:3 * BANK + T]
        ps_mg = ps[:, 4 * BANK:4 * BANK + T * D].rearrange("p (t c) -> p t c", c=D)
        ps_v = ps[:, 5 * BANK:5 * BANK + T * 2 * D].rearrange("p (t c) -> p t c", c=2 * D)
        assert T * D <= BANK and T * 2 * D <= 2 * BANK
        ps_cnt = [ps[:, e * BANK:e * BANK + NB] for e in range(2)]
        ps_pre, ps_tot = ps[:, 2 * BANK:2 * BANK + NB], ps[:, 3 * BANK:3 * BANK + NB]
        ps_span = ps[:, 0:NB * D]
        ps_nt = ps[:, 0:NG * P]
        ps_nh = ps[:, 4 * BANK:4 * BANK + NG * P]

        edges_cleared, edges_loaded = sem("edges_cleared"), sem("edges_loaded")
        weights_cleared, weights_loaded = sem("weights_cleared"), sem("weights_loaded")
        node_cleared, node_loaded = sem("node_cleared"), sem("node_loaded")
        zeros_ready, dram_cleared = sem("zeros_ready"), sem("dram_cleared")
        consts_ready, pool_made = sem("consts_ready"), sem("pool_made")
        hot_ready, hot_free, counted = sem("hot_ready"), sem("hot_free"), sem("counted")
        prefix_in, prefix_out = sem("prefix_in"), sem("prefix_out")
        sqrt_in, sqrt_out = sem("sqrt_in"), sem("sqrt_out")
        table_ready = [sem(f"table_ready{l}") for l in range(3)]
        table_stored = [sem(f"table_stored{l}") for l in range(3)]
        starts_put, first_row = sem("starts_put"), sem("first_row")
        xd_loaded, xd_spread = sems("xd_loaded"), sem("xd_spread")
        idx_ready = [sem(f"idx_ready{l}") for l in range(3)]
        gathered = [sems(f"gathered{l}_") for l in range(3)]
        sums_ready = [sem(f"sums_ready{l}") for l in range(3)]
        sums_stored = [sems(f"sums_stored{l}_") for l in range(3)]
        span_in = [sem(f"span_in{l}") for l in range(3)]
        span_out = [sem(f"span_out{l}") for l in range(3)]
        ends_got = [sem(f"ends_got{l}") for l in range(3)]
        xt_ready, xt_copied, h_ready, h_done = sem("xt_ready"), sem("xt_copied"), sem("h_ready"), sem("h_done")
        row_ready, same_ready, lead_ready = sem("row_ready"), sem("same_ready"), sem("lead_ready")
        v_ready, msgs_ready = sem("v_ready"), sem("msgs_ready")
        merge_ready, merged_ready = sem("merge_ready"), sem("merged_ready")
        scattered = sems("scattered")
        acc_loaded = sem("acc_loaded")
        pool_turn = sem("pool_turn")
        nt_in, nt_ready, nt_copied, nh_ready = sem("nt_in"), sem("nt_ready"), sem("nt_copied"), sem("nh_ready")
        tanh_in, tanh_out = sem("tanh_in"), sem("tanh_out")
        out_ready, out_stored = sem("out_ready"), sem("out_stored")
        dve_done = sem("dve_done")

        by_lo = "(h l) c -> l h c"
        src_v = src.rearrange("(p t) -> p t", p=P)
        dst_v = dst.rearrange("(p t) -> p t", p=P)
        xd_v = xd_rows.rearrange("(p t) c -> p t c", p=P)
        runsum_v = [r.rearrange("(p t) c -> p t c", p=P) for r in runsums]

        block = ctx.enter_context(nc.Block())

        @block.sync
        def _(sp):
            sp.wait_ge(edges_cleared, 1)
            sp.dma_start(src_i[:, 0:EP], src_v).then_inc(edges_loaded, 16)
            sp.dma_start(dst_i, dst_v).then_inc(edges_loaded, 16)
            sp.dma_start(prev_last[1:P, :], dst_v[0:P - 1, EP - 1:EP]).then_inc(edges_loaded, 16)
            sp.dma_start(next_first[0:P - 1, :], dst_v[1:P, 0:1]).then_inc(edges_loaded, 16)
            sp.wait_ge(node_cleared, 1)
            sp.dma_start(node_x[:, 0:NB - 1, :], x[0:(NB - 1) * P, :].rearrange(by_lo, l=P)).then_inc(node_loaded, 16)
            sp.dma_start(node_x[0:TAIL, NB - 1, :], x[(NB - 1) * P:N, :]).then_inc(node_loaded, 16)

            sp.wait_ge(table_ready[0], 1)
            sp.dma_start(table0.rearrange(by_lo, l=P), node_tab[:, :, 0:R]).then_inc(table_stored[0], 16)
            sp.wait_ge(starts_put, 16 * NB)
            for k in range(SLOTS):
                sp.dma_start(xd_in[:, k], xd_v[:, k * T:(k + 1) * T, :]).then_inc(xd_loaded[k], 16)
                sp.sem_inc(sums_stored[0][k], 16)
            with sp.Fori(0, ITERS - 1) as i:
                for k in range(SLOTS):
                    sp.wait_ge(xd_spread, i * SLOTS + (k + 1))
                    sp.dma_start(xd_in[:, k], xd_v[:, bass.ds(i * STEP + (STEP + k * T), T), :]).then_inc(xd_loaded[k], 16)
                    sp.wait_ge(sums_ready[0], i * SLOTS + (k + 1))
                    sp.dma_start(runsum_v[0][:, bass.ds(i * STEP + k * T, T), :], sums[:, k]).then_inc(sums_stored[0][k], 16)
            for k in range(SLOTS):
                g = (ITERS - 1) * SLOTS + k
                sp.wait_ge(sums_ready[0], g + 1)
                sp.dma_start(runsum_v[0][:, g * T:(g + 1) * T, :], sums[:, k]).then_inc(sums_stored[0][k], 16)
            for k in range(SLOTS):
                sp.wait_ge(scattered[k], 16 * T * ITERS)
            sp.wait_ge(merged_ready, ITERS * SLOTS)
            for c in range(COPIES):
                sp.dma_start(acc_in[c], src_sums[c].rearrange(by_lo, l=P)).then_inc(acc_loaded, 16)

            for l in (1, 2):
                sp.wait_ge(table_ready[l], 1)
                sp.dma_start(tables[l - 1].rearrange(by_lo, l=P), node_t[:, :, :]).then_inc(table_stored[l], 16)
                for k in range(SLOTS):
                    sp.sem_inc(sums_stored[l][k], 16)
                with sp.Fori(0, ITERS) as i:
                    for k in range(SLOTS):
                        sp.wait_ge(sums_ready[l], i * SLOTS + (k + 1))
                        sp.dma_start(runsum_v[l][:, bass.ds(i * STEP + k * T, T), :], sums[:, k]).then_inc(sums_stored[l][k], 16)

            sp.wait_ge(out_ready, 1)
            sp.dma_start(out[0:(NB - 1) * P, :].rearrange(by_lo, l=P), agg[:, 0:NB - 1, :]).then_inc(out_stored, 16)
            sp.dma_start(out[(NB - 1) * P:N, :], agg[0:TAIL, NB - 1, :]).then_inc(out_stored, 16)
            sp.wait_ge(out_stored, 32)

        @block.gpsimd
        def _(pool):
            pool.memset(ident[:, :], 0.0).then_inc(pool_made, 1)
            pool.memset(before[:, :], 1.0).then_inc(pool_made, 1)
            pool.iota(iota_lo[:, :, :], pattern=[[1, P], [0, T]], base=0, channel_multiplier=0,
                      allow_small_or_imprecise_dtypes=True)
            pool.iota(iota_f[:, :], pattern=[[1, P]], base=0, channel_multiplier=0,
                      allow_small_or_imprecise_dtypes=True)
            pool.iota(pow_i[:, :], pattern=[[0, 1]], base=127 + 63, channel_multiplier=-1)
            pool.wait_ge(pool_made, 2)
            pool.affine_select(out=ident[:, :], in_=ident[:, :], compare_op=ALU.not_equal, fill=1.0,
                               base=0, pattern=[[-1, P]], channel_multiplier=1)
            pool.affine_select(out=before[:, :], in_=before[:, :], compare_op=ALU.is_gt, fill=0.0,
                               base=0, pattern=[[1, P]], channel_multiplier=-1).then_inc(consts_ready, 1)

            def hold(semaphore, value):
                pool.wait_ge(semaphore, value)
                pool.sem_inc(pool_turn, 1)

            def gather(into, table, index):
                return pool.indirect_dma_start(out=into, out_offset=None, in_=table,
                                               in_offset=bass.IndirectOffsetOnAxis(index, 0))

            pool.wait_ge(table_stored[0], 16)
            pool.wait_ge(dram_cleared, 16 * (ITERS + COPIES))
            for h in range(NB):
                pool.indirect_dma_start(
                    out=xd_rows, out_offset=bass.IndirectOffsetOnAxis(start_i[:, h:h + 1], 0),
                    in_=node_tab[:, h, 1:R + 1], in_offset=None, bounds_check=E - 1, oob_is_err=False,
                ).then_inc(starts_put, 16)
            gather(first_tab[:, :], table0, first_i[:, :]).then_inc(first_row, 16)

            def gather_sources(k, j):
                for t in range(j * BATCH, (j + 1) * BATCH):
                    gather(xsd[:, k, t, 0:R], table0, idx[:, k, t:t + 1]).then_inc(gathered[0][k], 16)

            def scatter_messages(k, j):
                for t in range(j * BATCH, (j + 1) * BATCH):
                    pool.indirect_dma_start(
                        out=src_sums[t % COPIES], out_offset=bass.IndirectOffsetOnAxis(put_i[:, k, t:t + 1], 0),
                        in_=merged[:, k, t, :], in_offset=None, bounds_check=NPAD - 1, oob_is_err=False,
                        compute_op=ALU.add).then_inc(scattered[k], 16)

            LAG = 2
            for k in range(SLOTS):
                pool.wait_ge(idx_ready[0], k + 1)
                for j in range(BATCHES):
                    gather_sources(k, j)
                    if k >= LAG:
                        b = k - LAG
                        if j == 0:
                            pool.wait_ge(merged_ready, b + 1)
                        if j > 0:
                            pool.wait_ge(scattered[b], 16 * BATCH * j)
                        elif b > 0:
                            pool.wait_ge(scattered[b - 1], 16 * T)
                        scatter_messages(b, j)
            with pool.Fori(1, ITERS) as i:
                for k in range(SLOTS):
                    hold(idx_ready[0], i * SLOTS + (k + 1))
                    for j in range(BATCHES):
                        gather_sources(k, j)
                        b = (k - LAG) % SLOTS
                        back = SLOTS if k < LAG else 0
                        if j == 0:
                            hold(merged_ready, i * SLOTS + (b + 1 - back))
                            a = (b - 1) % SLOTS
                            turns = i * (16 * T) + (16 * T if b > 0 and not back else 0)
                            if back and b == 0:
                                turns = i * (16 * T) - 16 * T
                            hold(scattered[a], turns)
                        else:
                            hold(scattered[b], i * (16 * T) + (16 * BATCH * j - (16 * T if back else 0)))
                        scatter_messages(b, j)
            for b in range(SLOTS - LAG, SLOTS):
                pool.wait_ge(merged_ready, (ITERS - 1) * SLOTS + b + 1)
                for j in range(BATCHES):
                    if j > 0:
                        pool.wait_ge(scattered[b], 16 * T * (ITERS - 1) + 16 * BATCH * j)
                    else:
                        pool.wait_ge(scattered[b - 1], 16 * T * ITERS)
                    scatter_messages(b, j)

            def gather_ends(l):
                for k in range(SLOTS):
                    pool.wait_ge(sums_stored[l][k], 16 * (ITERS + 1))
                for h in range(NB):
                    gather(agg[:, h, :], runsums[l], end_i[:, h:h + 1]).then_inc(ends_got[l], 16)

            gather_ends(0)
            for l in (1, 2):
                pool.wait_ge(table_stored[l], 16)
                with pool.Fori(0, ITERS) as i:
                    for k in range(SLOTS):
                        hold(idx_ready[l], i * SLOTS + (k + 1))
                        for t in range(T):
                            gather(rows[:, k, t, :], tables[l - 1], idx[:, k, t:t + 1]).then_inc(gathered[l][k], 16)
                gather_ends(l)

        @block.scalar
        def _(act):
            act.wait_ge(weights_cleared, 1)
            w1_t = mlp_w1.rearrange("o f -> f o")
            w2_t = mlp_w2.rearrange("o f -> f o")
            n = 0
            for to, of in (
                (w1c[:, 0:HID], w1_t), (w1c[0:D, HID:P], w1_t[D:2 * D, :]), (w1c[D:2 * D, HID:P], w1_t[0:D, :]),
                (b1c[0:HID, :], mlp_b1.rearrange("(o a) -> o a", a=1)),
                (b1c[HID:P, :], mlp_b1.rearrange("(o a) -> o a", a=1)),
                (w2c[0:HID, 0:D], w2_t), (w2c[HID:P, D:2 * D], w2_t),
                (b2c[:, 0:D], mlp_b2.partition_broadcast(P)), (b2c[:, D:2 * D], mlp_b2.partition_broadcast(P)),
                (gcn_b[0][:, :], gcn_b1.partition_broadcast(P)), (gcn_b[1][:, :], gcn_b2.partition_broadcast(P)),
                *((gcn_w[l][b * D:(b + 1) * D, b * D:(b + 1) * D], w)
                  for l, w in enumerate((gcn_w1, gcn_w2)) for b in range(PER)),
            ):
                act.dma_start(to, of).then_inc(weights_loaded, 16)
                n += 1
            assert n == 11 + 2 * PER
            act.wait_ge(zeros_ready, 1)
            for i in range(ITERS):
                act.dma_start(xd_v[:, i * STEP:(i + 1) * STEP, :],
                              zeros[:, :].rearrange("p (t c) -> p t c", c=R)).then_inc(dram_cleared, 16)
            for c in range(COPIES):
                act.dma_start(src_sums[c].rearrange("(p h) c -> p (h c)", p=P), zeros[:, 0:NB * D]).then_inc(dram_cleared, 16)

            def root(n):
                act.wait_ge(sqrt_in, n)
                act.activation(st[1][:, :], st[0][:, :], ACT.Sqrt).then_inc(sqrt_out, 1)

            root(1)
            root(2)
            act.wait_ge(weights_loaded, 16 * (11 + 2 * PER))
            with act.Fori(0, ITERS * SLOTS) as g:
                for j, cols in enumerate(PARTS):
                    w = len(cols) * P
                    act.wait_ge(xt_ready, g * SUBS + (j + 1))
                    act.activation(xt[:, 0:w], ps_xt[:, 0:w], ACT.Copy).then_inc(xt_copied, 1)
                    act.wait_ge(h_ready, g * SUBS + (j + 1))
                    act.activation(hid[:, 0:w], ps_h[:, 0:w], ACT.Relu, bias=b1c[:, :]).then_inc(h_done, 1)
            root(3)
            for l in (1, 2):
                act.wait_ge(nt_ready, l)
                for c in range(0, NG * P, BANK):
                    e = min(c + BANK, NG * P)
                    last = act.activation(node_xt[:, c:e], ps_nt[:, c:e], ACT.Copy)
                last.then_inc(nt_copied, 1)
                act.wait_ge(tanh_in, l)
                act.activation(node_h[:, 0:NB, :], agg[:, :, :], ACT.Tanh).then_inc(tanh_out, 1)
            root(4)

        @block.tensor
        def _(pe):
            pe.wait_ge(zeros_ready, 1)
            for e in range(2):
                nc.tensor.matmul(ps_cnt[e], zeros[:, 0:P], zeros[:, 0:NB], start=True, stop=False)
            with pe.Fori(0, ITERS * SLOTS) as i:
                for e in range(2):
                    pe.wait_ge(hot_ready, i * 2 + (e + 1))
                    for t in range(T):
                        last = nc.tensor.matmul(ps_cnt[e], hot_lo[e][:, :, t], hot_hi[e][:, :, t], start=False, stop=False)
                    last.then_inc(hot_free, 1)
            for e in range(2):
                last = nc.tensor.matmul(ps_cnt[e], zeros[:, 0:P], zeros[:, 0:NB], start=False, stop=True)
            last.then_inc(counted, 1)
            pe.wait_ge(consts_ready, 1)
            pe.wait_ge(prefix_in, 1)
            nc.tensor.matmul(ps_pre, before[:, :], cnt[:, 1, :], start=True, stop=True)
            nc.tensor.matmul(ps_tot, ones[:, :], cnt[:, 1, :], start=True, stop=True).then_inc(prefix_out, 1)

            pe.wait_ge(weights_loaded, 16 * (11 + 2 * PER))
            with pe.Fori(0, ITERS) as i:
                for k in range(SLOTS):
                    pe.wait_ge(gathered[0][k], i * (16 * T) + 16 * T)
                    pe.wait_ge(xd_spread, i * SLOTS + (k + 1))
                    for j, cols in enumerate(PARTS):
                        at = k * SUBS + j + 1
                        for u, t in enumerate(cols):
                            last = nc.tensor.transpose(ps_xt[:, u * P:(u + 1) * P], xsd[:, k, t, 1:1 + 2 * D], ident[:, :])
                        last.then_inc(xt_ready, 1)
                        for u, t in enumerate(cols):
                            last = nc.tensor.matmul(ps_eq[:, u, :], src_f[:, k, t:t + 1].to_broadcast([P, P]), ident[:, :],
                                                    start=True, stop=True)
                        last.then_inc(row_ready, 1)
                        pe.wait_ge(xt_copied, i * (SLOTS * SUBS) + at)
                        w = len(cols) * P
                        nc.tensor.matmul(ps_h[:, 0:w], w1c[:, :], xt[:, 0:w], start=True, stop=True).then_inc(h_ready, 1)
                        pe.wait_ge(h_done, i * (SLOTS * SUBS) + at)
                        for u, t in enumerate(cols):
                            last = nc.tensor.matmul(ps_v[:, t, :], hid[:, u * P:(u + 1) * P], w2c[:, :], start=True, stop=True)
                        if j == SUBS - 1:
                            last.then_inc(v_ready, 1)
                        pe.wait_ge(same_ready, i * (SLOTS * SUBS) + at)
                        for t in cols:
                            last = nc.tensor.matmul(ps_ld[:, t:t + 1], same[:, t, :], pow2, start=True, stop=True)
                        if j == SUBS - 1:
                            last.then_inc(lead_ready, 1)
                    pe.wait_ge(msgs_ready, i * SLOTS + (k + 1))
                    for t in range(T):
                        last = nc.tensor.matmul(ps_mg[:, t, :], same[:, t, :], msgs[:, t, 0, :], start=True, stop=True)
                    last.then_inc(merge_ready, 1)

            def spans(l):
                pe.wait_ge(span_in[l], 1)
                flat = tmp[:, :, :].rearrange("p h c -> p (h c)")
                for c in range(0, NB * D, BANK):
                    e = min(c + BANK, NB * D)
                    last = nc.tensor.matmul(ps_span[:, c:e], last_lo[:, :], flat[:, c:e], start=True, stop=True)
                last.then_inc(span_out[l], 1)

            spans(0)
            for l in (1, 2):
                pe.wait_ge(nt_in, l)
                flat = node_h[:, :, :].rearrange("p h c -> p (h c)")
                for b in range(NG):
                    last = nc.tensor.transpose(ps_nt[:, b * P:(b + 1) * P], flat[:, b * P:(b + 1) * P], ident[:, :])
                last.then_inc(nt_ready, 1)
                pe.wait_ge(nt_copied, l)
                for b in range(NG):
                    last = nc.tensor.matmul(ps_nh[:, b * P:(b + 1) * P], node_xt[:, b * P:(b + 1) * P], gcn_w[l - 1][:, :],
                                            start=True, stop=True)
                last.then_inc(nh_ready, 1)
                spans(l)

        @block.vector
        def _(dve):
            v = nc.vector
            done = [0]
            base = [0]

            def step(ins):
                done[0] += 1
                ins.then_inc(dve_done, 1)
                dve.wait_ge(dve_done, base[0] + done[0])

            v.memset(prev_last[:, :], -1)
            v.memset(src_i[:, EP:], 0)
            v.memset(keep[:, EP:], 0.0)
            v.memset(next_first[:, :], -1).then_inc(edges_cleared, 1)
            v.memset(gcn_w[0][:, :], 0.0)
            v.memset(gcn_w[1][:, :], 0.0)
            v.memset(w2c[:, :], 0.0).then_inc(weights_cleared, 1)
            v.memset(node_x[:, :, :], 0.0).then_inc(node_cleared, 1)
            v.memset(zeros[:, :], 0.0).then_inc(zeros_ready, 1)
            v.memset(ones[:, :], 1.0)
            step(v.memset(node_h[:, :, :], 0.0))
            dve.wait_ge(consts_ready, 1)
            step(v.tensor_scalar(pow2_i[:, :], pow_i[:, :], 23, None, ALU.logical_shift_left))
            step(v.tensor_scalar(lead_max[:, :], pow2, 2.0, None, ALU.mult))

            dve.wait_ge(edges_loaded, 16 * 4)
            for e, ends in enumerate((src_i[:, 0:EP], dst_i)):
                step(v.tensor_scalar(split_i, ends, P - 1, None, ALU.bitwise_and))
                step(v.tensor_copy(lohi[e][0], split_i))
                step(v.tensor_scalar(split_i, ends, P.bit_length() - 1, None, ALU.arith_shift_right))
                step(v.tensor_copy(lohi[e][1], split_i))
            v.tensor_tensor(keep[:, 1:EP], dst_i[:, 1:EP], dst_i[:, 0:EP - 1], ALU.is_equal)
            v.tensor_tensor(keep[:, 0:1], dst_i[:, 0:1], prev_last[:, :], ALU.is_equal)
            v.tensor_tensor(runs_on[:, :], dst_i[:, EP - 1:EP], next_first[:, :], ALU.is_equal)
            v.tensor_copy(first_i[:, :], dst_i[:, 0:1])
            v.tensor_scalar(last_lohi_i[:, 0:1], dst_i[:, EP - 1:EP], P - 1, None, ALU.bitwise_and)
            step(v.tensor_scalar(last_lohi_i[:, 1:2], dst_i[:, EP - 1:EP], P.bit_length() - 1, None, ALU.arith_shift_right))
            step(v.tensor_copy(last_lohi[:, :], last_lohi_i[:, :]))
            v.tensor_scalar(last_lo[:, :], iota_f[:, :], last_lohi[:, 0:1], None, ALU.is_equal)
            step(v.tensor_scalar(last_hi[:, :], iota_f[:, 0:NB], last_lohi[:, 1:2], None, ALU.is_equal))

            def one_hots(e, col):
                lo = lohi[e][0][:, bass.ds(col, T)].unsqueeze(1)
                hi = lohi[e][1][:, bass.ds(col, T)].unsqueeze(1)
                v.tensor_tensor(hot_lo[e], lo.to_broadcast([P, P, T]), iota_lo[:, :, :], ALU.is_equal)
                v.tensor_tensor(hot_hi[e], hi.to_broadcast([P, NB, T]), iota_lo[:, 0:NB, :], ALU.is_equal).then_inc(hot_ready, 1)

            for e in range(2):
                one_hots(e, 0)
            with dve.Fori(1, ITERS * SLOTS) as i:
                for e in range(2):
                    dve.wait_ge(hot_free, i * 2 + (e - 1))
                    one_hots(e, i * T)
            dve.wait_ge(counted, 1)
            for e in range(2):
                last = v.tensor_copy(cnt[:, e, :], ps_cnt[e])
            step(last)

            def rsqrt(n, to, arg):
                dve.wait_ge(sqrt_out, n)
                step(v.reciprocal(st[2][:, :], st[1][:, :]))
                step(v.tensor_tensor(st[3][:, :], st[2][:, :], st[2][:, :], ALU.mult))
                step(v.tensor_tensor(st[3][:, :], st[3][:, :], arg, ALU.mult))
                step(v.tensor_scalar(st[3][:, :], st[3][:, :], -0.5, 1.5, ALU.mult, ALU.add))
                step(v.tensor_tensor(to, st[2][:, :], st[3][:, :], ALU.mult))

            step(v.tensor_tensor(st[0][:, :], cnt[:, 0, :], cnt[:, 1, :], ALU.add))
            v.tensor_scalar(st[0][:, :], st[0][:, :], DEG_MIN, None, ALU.max).then_inc(sqrt_in, 1)
            dve.wait_ge(sqrt_in, 1)
            rsqrt(1, dis[:, :], st[0][:, :])
            v.tensor_scalar(st[0][:, :], cnt[:, 1, :], 1.0, None, ALU.add).then_inc(sqrt_in, 1)
            dve.wait_ge(sqrt_in, 2)
            rsqrt(2, dinv[:, :], st[0][:, :])
            v.tensor_scalar(has_in[:, :], cnt[:, 1, :], 0.0, None, ALU.is_gt).then_inc(prefix_in, 1)
            dve.wait_ge(prefix_out, 1)
            step(v.tensor_copy(st[0][:, :], ps_tot))
            step(v.tensor_tensor_scan(total[:, :], ones[:, 0:NB], st[0][:, :], 0.0, ALU.mult, ALU.add))
            step(v.tensor_tensor(total[:, :], total[:, :], st[0][:, :], ALU.subtract))
            step(v.tensor_tensor(start[:, :], ps_pre, total[:, :], ALU.add))
            step(v.tensor_tensor(st[0][:, :], start[:, :], cnt[:, 1, :], ALU.add))
            step(v.tensor_scalar(end_i[:, :], st[0][:, :], -1.0, 0.0, ALU.add, ALU.max))
            dve.wait_ge(prefix_in, 1)
            step(v.tensor_scalar(st[1][:, :], has_in[:, :], -float(FAR), float(FAR), ALU.mult, ALU.add))
            step(v.tensor_tensor(start_i[:, :], st[1][:, :], start[:, :], ALU.add))
            dve.wait_ge(node_loaded, 32)
            v.tensor_copy(node_tab[:, :, 1:R], node_x[:, 0:NB, :])
            v.tensor_copy(node_tab[:, :, R:R + 1], dis[:, :].unsqueeze(2))
            v.tensor_copy(node_tab[:, :, 0:1], dis[:, :].unsqueeze(2)).then_inc(table_ready[0], 1)

            def stage(l, k, col):
                if l == 0:
                    v.tensor_copy(src_f[:, k, :], src_i[:, bass.ds(col, T)])
                v.tensor_copy(keep_s[:, k, :], keep[:, bass.ds(col, T)])
                v.tensor_copy(idx[:, k, :], src_i[:, bass.ds(col, T)]).then_inc(idx_ready[l], 1)

            def running_sums(l, k, i, values):
                dve.wait_ge(sums_stored[l][k], i * 16 + 16)
                for c in range(D):
                    last = v.tensor_tensor_scan(sums[:, k, :, c], keep_s[:, k, :], values(c),
                                                sums[:, (k - 1) % SLOTS, T - 1, c:c + 1], ALU.mult, ALU.add)
                last.then_inc(sums_ready[l], 1)
                dve.wait_ge(sums_ready[l], i * SLOTS + (k + 1))

            def clear_carry(l):
                step(v.memset(sums[:, SLOTS - 1, T - 1, :], 0.0))
                for k in range(SLOTS):
                    stage(l, k, k * T)
                dve.wait_ge(idx_ready[l], SLOTS)

            clear_carry(0)
            dve.wait_ge(weights_loaded, 16 * (11 + 2 * PER))
            dve.wait_ge(first_row, 16)
            v.tensor_copy(xsd[:, SLOTS - 1, T - 1, R:R + D], first_tab[:, 1:R])
            step(v.tensor_copy(xsd[:, SLOTS - 1, T - 1, R + D:2 * R], first_tab[:, 0:1]))
            LINKS = 17
            before_loop = done[0]
            with dve.Fori(0, ITERS) as i:
                done[0], base[0] = 0, i * (LINKS * SLOTS) + before_loop
                for k in range(SLOTS):
                    g1 = i * SLOTS + (k + 1)
                    dve.wait_ge(xd_loaded[k], i * 16 + 16)
                    for c in range(R):
                        last = v.tensor_tensor_scan(xsd[:, k, :, R + c], keep_s[:, k, :], xd_in[:, k, :, c],
                                                    xsd[:, (k - 1) % SLOTS, T - 1, R + c:R + c + 1], ALU.mult, ALU.add)
                    last.then_inc(xd_spread, 1)
                    for j, part in enumerate(PARTS):
                        dve.wait_ge(row_ready, i * (SLOTS * SUBS) + (k * SUBS + j + 1))
                        cols, w = slice(part.start, part.stop), len(part)
                        v.tensor_tensor(same[:, cols, :], ps_eq[:, 0:w, :],
                                        src_f[:, k, cols].unsqueeze(2).to_broadcast([P, w, P]),
                                        ALU.is_equal).then_inc(same_ready, 1)
                    dve.wait_ge(xd_spread, g1)
                    wide = [P, T, 2, D]
                    step(v.tensor_tensor(xw, xsd[:, k, :, 1:1 + 2 * D].rearrange("p t (s c) -> p t s c", s=2),
                                         xsd[:, k, :, 0:2 * R:2 * R - 1].unsqueeze(3).to_broadcast(wide), ALU.mult))
                    dve.wait_ge(v_ready, g1)
                    step(v.tensor_tensor(refl.rearrange("p t s c -> p t (s c)"), ps_v,
                                         b2c[:, :].unsqueeze(1).to_broadcast([P, T, 2 * D]), ALU.add))
                    step(v.tensor_tensor(prod, refl, refl, ALU.mult))
                    step(v.tensor_reduce(scale2, prod, AX.X, ALU.add))
                    step(v.tensor_scalar(scale2, scale2, NORM_MIN, 0.5, ALU.max, ALU.mult))
                    step(v.reciprocal(scale2, scale2))

                    def dot_scaled():
                        step(v.tensor_reduce(dots, prod, AX.X, ALU.add))
                        step(v.tensor_tensor(dots, dots, scale2, ALU.mult))
                        step(v.tensor_tensor(prod, refl, dots.unsqueeze(3).to_broadcast(wide), ALU.mult))

                    step(v.tensor_tensor(prod, refl, xw, ALU.mult))
                    dot_scaled()
                    step(v.tensor_tensor(mirrored, xw, prod, ALU.subtract))
                    for s in range(2):
                        last = v.tensor_tensor(prod[:, :, s, :], refl[:, :, s, :], mirrored[:, :, 1 - s, :], ALU.mult)
                    step(last)
                    dot_scaled()
                    for s in range(2):
                        last = v.tensor_tensor(msgs[:, :, s, :], mirrored[:, :, 1 - s, :], prod[:, :, s, :], ALU.subtract)
                    last.then_inc(msgs_ready, 1)
                    dve.wait_ge(msgs_ready, g1)
                    running_sums(0, k, i, lambda c: msgs[:, :, 1, c])
                    dve.wait_ge(lead_ready, g1)
                    step(v.tensor_scalar(late, ps_ld, lead_max[:, :], float(SKIP), ALU.is_gt, ALU.mult))
                    step(v.tensor_tensor(put_i[:, k, :], late, src_f[:, k, :], ALU.add))
                    dve.wait_ge(merge_ready, g1)
                    v.tensor_copy(merged[:, k, :, :], ps_mg).then_inc(merged_ready, 1)
                    stage(0, k, i * STEP + (STEP + k * T))
                assert done[0] == LINKS * SLOTS, done[0]
            base[0], done[0] = 0, before_loop + ITERS * LINKS * SLOTS

            def node_sums(l):
                step(v.tensor_scalar(last_row[:, :], sums[:, SLOTS - 1, T - 1, :], runs_on[:, :], None, ALU.mult))
                v.tensor_tensor(tmp[:, :, :], last_hi[:, :].unsqueeze(2).to_broadcast([P, NB, D]),
                                last_row[:, :].unsqueeze(1).to_broadcast([P, NB, D]), ALU.mult).then_inc(span_in[l], 1)
                dve.wait_ge(ends_got[l], 16 * NB)
                step(v.tensor_tensor(agg[:, :, :], agg[:, :, :], has_in[:, :].unsqueeze(2).to_broadcast([P, NB, D]), ALU.mult))
                dve.wait_ge(span_out[l], 1)
                step(v.tensor_tensor(agg[:, :, :], agg[:, :, :], ps_span.rearrange("p (h c) -> p h c", c=D), ALU.add))

            def per_node(a):
                return a[:, :].unsqueeze(2).to_broadcast([P, NB, D])

            def layernorm(n, to, a):
                step(v.tensor_reduce(st[0][:, :], a, AX.X, ALU.add))
                step(v.tensor_scalar(st[0][:, :], st[0][:, :], 1.0 / D, None, ALU.mult))
                step(v.tensor_tensor(a, a, per_node(st[0]), ALU.subtract))
                step(v.tensor_tensor(tmp[:, :, :], a, a, ALU.mult))
                step(v.tensor_reduce(st[0][:, :], tmp[:, :, :], AX.X, ALU.add))
                v.tensor_scalar(st[0][:, :], st[0][:, :], 1.0 / D, LN_EPS, ALU.mult, ALU.add).then_inc(sqrt_in, 1)
                dve.wait_ge(sqrt_in, n)
                rsqrt(n, st[3][:, :], st[0][:, :])
                return v.tensor_tensor(to, a, per_node(st[3]), ALU.mult)

            node_sums(0)
            dve.wait_ge(acc_loaded, 16 * COPIES)
            for c in range(COPIES):
                step(v.tensor_tensor(agg[:, :, :], agg[:, :, :], acc_in[c], ALU.add))
            step(v.tensor_tensor(agg[:, :, :], agg[:, :, :], per_node(dis), ALU.mult))
            step(v.tensor_tensor(agg[:, :, :], agg[:, :, :], node_x[:, 0:NB, :], ALU.add))
            step(v.tensor_scalar(agg[:, :, :], agg[:, :, :], 0.0, None, ALU.max))
            step(v.tensor_tensor(agg[:, :, :], agg[:, :, :], node_x[:, 0:NB, :], ALU.add))
            step(layernorm(3, node_h[:, 0:NB, :], agg[:, :, :]))
            v.tensor_copy(node_x[:, 0:NB, :], node_h[:, 0:NB, :]).then_inc(nt_in, 1)

            for l in (1, 2):
                dve.wait_ge(nh_ready, l)
                v.tensor_tensor(node_t[:, :, :], ps_nh[:, 0:NB * D].rearrange("p (h c) -> p h c", c=D),
                                per_node(dinv), ALU.mult).then_inc(table_ready[l], 1)
                for k in range(SLOTS):
                    dve.wait_ge(sums_stored[l - 1][k], 16 * (ITERS + 1))
                clear_carry(l)
                with dve.Fori(0, ITERS) as i:
                    for k in range(SLOTS):
                        dve.wait_ge(gathered[l][k], i * (16 * T) + 16 * T)
                        running_sums(l, k, i, lambda c: rows[:, k, :, c])
                        stage(l, k, i * STEP + (STEP + k * T))
                node_sums(l)
                step(v.tensor_tensor(agg[:, :, :], agg[:, :, :], node_t[:, :, :], ALU.add))
                step(v.tensor_tensor(agg[:, :, :], agg[:, :, :], per_node(dinv), ALU.mult))
                v.tensor_tensor(agg[:, :, :], agg[:, :, :], gcn_b[l - 1][:, :].unsqueeze(1).to_broadcast([P, NB, D]),
                                ALU.add).then_inc(tanh_in, 1)
                dve.wait_ge(tanh_out, l)
                if l == 1:
                    dve.drain().then_inc(nt_in, 1)
            step(v.tensor_tensor(node_x[:, 0:NB, :], node_x[:, 0:NB, :], node_h[:, 0:NB, :], ALU.add))
            layernorm(4, agg[:, :, :], node_x[:, 0:NB, :]).then_inc(out_ready, 1)


_INS = ['x', 'src', 'dst', 'L0_gnn_W1', 'L0_gnn_b1', 'L0_gnn_W2', 'L0_gnn_b2',
        'L1_gnn_W1', 'L1_gnn_b1', 'L1_gnn_W2', 'L1_gnn_b2']


def kernel(**inputs):
    import numpy as _np
    import concourse.bacc as _bacc
    from concourse import mybir as _mybir
    from concourse.bass_utils import run_bass_kernel_spmd as _run

    nc = _bacc.Bacc("TRN2", target_bir_lowering=False, num_devices=1)
    arrays, args = {}, []
    for name in _INS:
        a = _np.ascontiguousarray(inputs[name])
        arrays[f"in_{name}_dram"] = a
        args.append(nc.dram_tensor(f"in_{name}_dram", a.shape, _mybir.dt.from_np(a.dtype), kind="ExternalInput").ap())
    args.append(nc.dram_tensor("out_0_dram", inputs["x"].shape, _mybir.dt.float32, kind="ExternalOutput").ap())
    gnn_kernel(nc, *args)
    r = _run(nc, [arrays], core_ids=[0])
    return r.results[0]["out_0_dram"]
```

```python
import numpy as np
import concourse.bass as bass
import concourse.mybir as mybir
from contextlib import ExitStack


def ceil_div(a, b):
    return -(-a // b)


def gnn_kernel(nc, x, src, dst, mlp_w1, mlp_b1, mlp_w2, mlp_b2, gcn_w1, gcn_b1, gcn_w2, gcn_b2, out):
    F32, I32, BF16, F16 = mybir.dt.float32, mybir.dt.int32, mybir.dt.bfloat16, mybir.dt.float16
    ALU, ACT, AX = mybir.AluOpType, mybir.ActivationFunctionType, mybir.AxisListType

    P = 128
    N, D = x.shape
    E = src.shape[0]
    HID = mlp_w1.shape[0]
    EP = E // P
    T = 25
    GROUPS = EP // T
    SLOTS = 4
    STEP = T * SLOTS
    ITERS = GROUPS // SLOTS
    TP = 8
    TD = T - TP
    QUAD, QUADS, PAIRS = 4, TP // 4, TP // 2
    CHUNK = EP // 25
    assert EP * P == E and GROUPS * T == EP and ITERS * SLOTS + 1 == GROUPS
    assert 2 * HID == P and 2 * D == 32 and EP % 25 == 0
    BANKS = 2
    BATCH = 5
    BATCHES = T // BATCH
    BANK = 512
    SUBS = ceil_div(T, BANK // P)
    PARTS = [range(j * T // SUBS, (j + 1) * T // SUBS) for j in range(SUBS)]
    assert all(len(c) * P <= BANK for c in PARTS)
    NB = ceil_div(N, P)
    PER = P // D
    NG = ceil_div(NB, PER)
    NBP = NG * PER
    NPAD = NB * P
    TAIL = N - (NB - 1) * P
    KT = PER
    NQ = NBP // KT
    R = D + 1
    COPIES = BATCH
    SKIP = 1 << 14
    FAR = 1 << 20
    assert SKIP >= NPAD and FAR >= E
    LN_EPS, DEG_MIN, NORM_MIN = 1e-5, 1e-5, 1e-24

    ctx = ExitStack()
    with ctx:
        ctx.enter_context(nc.allow_non_contiguous_dma(reason="small transposed weights"))

        def sb(name, shape, dt=F32):
            return ctx.enter_context(nc.sbuf_tensor(name, shape, dt))

        def sem(name):
            return ctx.enter_context(nc.semaphore(name))

        def sems(name):
            return [sem(f"{name}{k}") for k in range(SLOTS)]

        def dram(name, shape):
            return nc.dram_tensor(name, shape, F32, kind="Internal").ap()

        table0 = dram("table0", [NPAD, R])
        tables = [dram(f"table{l}", [NPAD, D]) for l in (1, 2)]
        xd_rows = dram("xd_rows", [E, R])
        runsums = [dram(f"runsum{l}", [E, D]) for l in range(3)]
        src_sums = [dram(f"src_sum{c}", [NPAD, D]) for c in range(COPIES)]

        src_i = sb("src_i", [P, EP + STEP], I32)
        low_h = sb("low_h", [P, EP + STEP], F16)
        high_h = sb("high_h", [P, EP + STEP], F16)
        keep = sb("keep", [P, EP + STEP], BF16)
        prev_last = sb("prev_last", [P, 1], I32)
        next_first = sb("next_first", [P, 1], I32)
        first_i = sb("first_i", [P, 1], I32)
        last_lohi_i = sb("last_lohi_i", [P, 2], I32)
        last_lohi = sb("last_lohi", [P, 2])
        runs_on = sb("runs_on", [P, 1])
        HOT_WORDS = QUADS * KT * QUAD * P // 2
        early = sb("early", [P, HOT_WORDS])
        hot = early[:, :].bitcast(BF16).rearrange("p (q c e) -> p q c e", q=QUADS, c=KT)
        zeros = early[:, 0:CHUNK * R]
        iota_lo = early[:, CHUNK * R + 1:CHUNK * R + 1 + P * T // 2].bitcast(BF16).rearrange("p (j t) -> p j t", t=T)
        assert CHUNK * R + 1 + P * T // 2 <= HOT_WORDS
        low_row = sb("low_row", [P, QUAD * P], F16)
        parts = sb("parts", [P, KT, 3, NQ * R], BF16)
        picked_sb = sb("picked_sb", [P, 2 * NQ * R])
        ident_h = sb("ident_h", [P, P], F16)
        slot_id = sb("slot_id", [P, KT])
        high_id = sb("high_id", [P, NQ], F16)
        iota_f = sb("iota_f", [P, P])
        ident = sb("ident", [P, P])
        before = sb("before", [P, P])
        ones = sb("ones", [P, P])
        pow_i = sb("pow_i", [P, 1], I32)
        pow2_i = sb("pow2_i", [P, 1], I32)
        pow2 = pow2_i[:, :].bitcast(F32)
        lead_max = sb("lead_max", [P, 1])
        w1c = sb("w1c", [2 * D, P])
        b1c = sb("b1c", [P, 1])
        w2c = sb("w2c", [P, 2 * D])
        b2c = sb("b2c", [P, 2 * D])
        gcn_w = [sb(f"gcn_w{l}", [P, P]) for l in (1, 2)]
        gcn_b = [sb(f"gcn_b{l}", [P, D]) for l in (1, 2)]

        WORDS = 2 * EP + T * P + T * NB + 64
        shared = sb("shared", [P, WORDS])
        half = shared[:, :].bitcast(BF16)
        lohi = [[half[:, (2 * e + h) * EP:(2 * e + h + 1) * EP] for h in range(2)] for e in range(2)]
        hot_at = 4 * EP
        hot_lo = [half[:, hot_at + e * P * T:hot_at + (e + 1) * P * T].rearrange("p (j t) -> p j t", t=T)
                  for e in range(2)]
        hot_at += 2 * P * T
        hot_hi = [half[:, hot_at + e * NB * T:hot_at + (e + 1) * NB * T].rearrange("p (j t) -> p j t", t=T)
                  for e in range(2)]
        split_i = shared[:, 2 * EP:3 * EP].bitcast(I32)
        same = shared[:, 0:T * P].bitcast(BF16).rearrange("p (b t e) -> p b t e", b=2, e=P)
        at = T * P
        pairs = []
        for _ in range(5):
            pairs.append(shared[:, at:at + T * 2 * D].rearrange("p (t s c) -> p t s c", t=T, s=2))
            at += T * 2 * D
        refl, xw, prod, mirrored, msgs = pairs
        dots = shared[:, at:at + 2 * T].rearrange("p (t s) -> p t s", s=2)
        scale2 = shared[:, at + 2 * T:at + 4 * T].rearrange("p (t s) -> p t s", s=2)
        late = shared[:, at + 4 * T:at + 5 * T]
        at += 5 * T
        PW = (0, R, R + D, R + 2 * D)
        msg_parts = shared[:, at:at + T * (PW[3] + 1) // 2].bitcast(BF16).rearrange("p (t c) -> p t c", t=T)
        assert at + T * (PW[3] + 1) // 2 <= WORDS and (PW[3] + 1) % 2 == 0
        acc_in = [shared[:, c * NB * D:(c + 1) * NB * D].rearrange("p (h c) -> p h c", c=D)
                  for c in range(COPIES)]
        node_xt = shared[:, COPIES * NB * D:COPIES * NB * D + NG * P]
        assert COPIES * NB * D + NG * P <= WORDS

        shared2 = sb("shared2", [P, max(2 * SLOTS * T * D, EP)])
        dst_i = shared2[:, 0:EP].bitcast(I32)
        sums = shared2[:, 0:SLOTS * T * D].rearrange("p (k t c) -> p k t c", k=SLOTS, t=T)
        merged = shared2[:, SLOTS * T * D:2 * SLOTS * T * D].rearrange("p (k t c) -> p k t c", k=SLOTS, t=T)

        idx = sb("idx", [P, SLOTS, T], I32)
        src_f = sb("src_f", [P, SLOTS, T])
        low_s = sb("low_s", [P, SLOTS, T], F16)
        high_s = sb("high_s", [P, SLOTS, T], F16)
        high_hot = sb("high_hot", [P, SLOTS, TP, NQ])
        keep_s = sb("keep_s", [P, SLOTS, T])
        put_i = sb("put_i", [P, SLOTS, T], I32)
        xsd = sb("xsd", [P, SLOTS, T, 2 * R])
        first_tab = sb("first_tab", [P, R])
        xd_in = sb("xd_in", [P, SLOTS, T, R])
        rows = xd_in[:, :, :, :].rearrange("p k t c -> p (k t c)")[:, 0:SLOTS * T * D].rearrange(
            "p (k t c) -> p k t c", k=SLOTS, t=T)
        xt = sb("xt", [2 * D, BANK])
        hid = sb("hid", [P, BANK])

        node_x = sb("node_x", [P, NBP, D])
        node_tab = sb("node_tab", [P, NBP, R + 1])
        node_t = node_tab[:, :, :].rearrange("p h c -> p (h c)")[:, 0:NBP * D].rearrange("p (h c) -> p h c", c=D)
        agg = sb("agg", [P, NB, D])
        wide_tmp = sb("wide_tmp", [P, NBP * R])
        tmp = wide_tmp[:, 0:NB * D].rearrange("p (h c) -> p h c", c=D)
        node_h = sb("node_h", [P, NBP, D])
        cnt = sb("cnt", [P, 2, NB])
        start = sb("start", [P, NB])
        total = sb("total", [P, NB])
        start_i = sb("start_i", [P, NB], I32)
        end_i = sb("end_i", [P, NB], I32)
        has_in = sb("has_in", [P, NB])
        dinv = sb("dinv", [P, NB])
        dis = sb("dis", [P, NB])
        st = [sb(f"st{i}", [P, NB]) for i in range(4)]
        last_hi = sb("last_hi", [P, NB])
        last_lo = sb("last_lo", [P, P])
        last_row = sb("last_row", [P, D])

        ps = ctx.enter_context(nc.psum_tensor("ps", [P, 8 * BANK], F32))
        ps_xt = ps[0:2 * D, 0:BANK]
        ps_eq = ps[:, BANK:2 * BANK].rearrange("p (t e) -> p t e", e=P)
        ps_h = ps[:, 2 * BANK:3 * BANK]
        ps_mg = ps[:, 3 * BANK:3 * BANK + T * R].rearrange("p (t c) -> p t c", c=R)
        ps_v = ps[:, 4 * BANK:4 * BANK + T * 2 * D].rearrange("p (t c) -> p t c", c=2 * D)
        ps_low = ps[:, 3 * BANK:4 * BANK]
        ps_pair = [ps[:, (6 + b) * BANK:(7 + b) * BANK] for b in range(BANKS)]
        assert T * R <= BANK and T * 2 * D <= 2 * BANK and 2 * NQ * R <= BANK and QUAD * P == BANK
        ps_cnt = [ps[:, e * BANK:e * BANK + NB] for e in range(2)]
        ps_pre, ps_tot = ps[:, 2 * BANK:2 * BANK + NB], ps[:, 3 * BANK:3 * BANK + NB]
        ps_span = ps[:, 0:NB * D]
        ps_nt = ps[:, 0:NG * P]
        ps_nh = ps[:, 4 * BANK:4 * BANK + NG * P]

        edges_cleared, edges_loaded = sem("edges_cleared"), sem("edges_loaded")
        weights_cleared, weights_loaded = sem("weights_cleared"), sem("weights_loaded")
        node_cleared, node_loaded = sem("node_cleared"), sem("node_loaded")
        zeros_ready, dram_cleared = sem("zeros_ready"), sem("dram_cleared")
        consts_ready, pool_made = sem("consts_ready"), sem("pool_made")
        hot_ready, hot_free, counted = sem("hot_ready"), sem("hot_free"), sem("counted")
        prefix_in, prefix_out = sem("prefix_in"), sem("prefix_out")
        sqrt_in, sqrt_out = sem("sqrt_in"), sem("sqrt_out")
        table_ready = [sem(f"table_ready{l}") for l in range(3)]
        table_stored = [sem(f"table_stored{l}") for l in range(3)]
        starts_put, first_row = sem("starts_put"), sem("first_row")
        xd_loaded, xd_spread = sems("xd_loaded"), sem("xd_spread")
        idx_ready = [sem(f"idx_ready{l}") for l in range(3)]
        gathered = [sems(f"gathered{l}_") for l in range(3)]
        sums_ready = [sem(f"sums_ready{l}") for l in range(3)]
        sums_stored = [sems(f"sums_stored{l}_") for l in range(3)]
        span_in = [sem(f"span_in{l}") for l in range(3)]
        span_out = [sem(f"span_out{l}") for l in range(3)]
        ends_got = [sem(f"ends_got{l}") for l in range(3)]
        xt_ready, xt_copied, h_ready, h_done = sem("xt_ready"), sem("xt_copied"), sem("h_ready"), sem("h_done")
        row_ready, same_ready = sem("row_ready"), sem("same_ready")
        v_ready, v_free, msgs_ready = sem("v_ready"), sem("v_free"), sem("msgs_ready")
        parts_ready = [sem(f"parts_ready{l}") for l in range(3)]
        low_ready = [sem(f"low_ready{l}") for l in range(3)]
        low_copied = [sem(f"low_copied{l}") for l in range(3)]
        slot_hot = [sem(f"slot_hot{l}") for l in range(3)]
        pair_ready = [sem(f"pair_ready{l}") for l in range(3)]
        pair_free = [sem(f"pair_free{l}") for l in range(3)]
        picked = [sem(f"picked{l}") for l in range(3)]
        merge_ready, merged_ready = sem("merge_ready"), sem("merged_ready")
        scattered = sems("scattered")
        acc_loaded = sem("acc_loaded")
        pool_turn = sem("pool_turn")
        nt_in, nt_ready, nt_copied, nh_ready = sem("nt_in"), sem("nt_ready"), sem("nt_copied"), sem("nh_ready")
        tanh_in, tanh_out = sem("tanh_in"), sem("tanh_out")
        out_ready, out_stored = sem("out_ready"), sem("out_stored")
        dve_done = sem("dve_done")

        by_lo = "(h l) c -> l h c"
        src_v = src.rearrange("(p t) -> p t", p=P)
        dst_v = dst.rearrange("(p t) -> p t", p=P)
        xd_v = xd_rows.rearrange("(p t) c -> p t c", p=P)
        runsum_v = [r.rearrange("(p t) c -> p t c", p=P) for r in runsums]

        block = ctx.enter_context(nc.Block())

        @block.sync
        def _(sp):
            sp.wait_ge(edges_cleared, 1)
            sp.dma_start(src_i[:, 0:EP], src_v).then_inc(edges_loaded, 16)
            sp.dma_start(dst_i, dst_v).then_inc(edges_loaded, 16)
            sp.dma_start(prev_last[1:P, :], dst_v[0:P - 1, EP - 1:EP]).then_inc(edges_loaded, 16)
            sp.dma_start(next_first[0:P - 1, :], dst_v[1:P, 0:1]).then_inc(edges_loaded, 16)
            sp.wait_ge(node_cleared, 1)
            sp.dma_start(node_x[:, 0:NB - 1, :], x[0:(NB - 1) * P, :].rearrange(by_lo, l=P)).then_inc(node_loaded, 16)
            sp.dma_start(node_x[0:TAIL, NB - 1, :], x[(NB - 1) * P:N, :]).then_inc(node_loaded, 16)

            sp.wait_ge(table_ready[0], 1)
            sp.dma_start(table0.rearrange(by_lo, l=P), node_tab[:, 0:NB, 0:R]).then_inc(table_stored[0], 16)
            sp.wait_ge(starts_put, 16 * NB)
            for k in range(SLOTS):
                sp.dma_start(xd_in[:, k], xd_v[:, k * T:(k + 1) * T, :]).then_inc(xd_loaded[k], 16)
                sp.sem_inc(sums_stored[0][k], 16)

            def load_rows(i, k):
                sp.wait_ge(xd_spread, i * SLOTS + (k + 1))
                sp.dma_start(xd_in[:, k], xd_v[:, bass.ds(i * STEP + (STEP + k * T), T), :]).then_inc(xd_loaded[k], 16)

            def store_sums(l, i, k):
                sp.wait_ge(sums_ready[l], i * SLOTS + (k + 1))
                sp.dma_start(runsum_v[l][:, bass.ds(i * STEP + k * T, T), :], sums[:, k]).then_inc(sums_stored[l][k], 16)

            with sp.Fori(0, ITERS - 1) as i:
                for k in range(SLOTS):
                    load_rows(i, k)
                    store_sums(0, i, k)
            load_rows(ITERS - 1, 0)
            for k in range(SLOTS):
                store_sums(0, ITERS - 1, k)
            store_sums(0, ITERS, 0)
            sp.wait_ge(merged_ready, GROUPS + 1)
            for b in range(SLOTS):
                sp.wait_ge(scattered[b], 16 * T * (ITERS + (b == 0)))
            for c in range(COPIES):
                sp.dma_start(acc_in[c], src_sums[c].rearrange(by_lo, l=P)).then_inc(acc_loaded, 16)

            for l in (1, 2):
                sp.wait_ge(table_ready[l], 1)
                sp.dma_start(tables[l - 1].rearrange(by_lo, l=P), node_t[:, 0:NB, :]).then_inc(table_stored[l], 16)
                for k in range(SLOTS):
                    sp.sem_inc(sums_stored[l][k], 16)
                with sp.Fori(0, ITERS) as i:
                    for k in range(SLOTS):
                        store_sums(l, i, k)
                store_sums(l, ITERS, 0)

            sp.wait_ge(out_ready, 1)
            sp.dma_start(out[0:(NB - 1) * P, :].rearrange(by_lo, l=P), agg[:, 0:NB - 1, :]).then_inc(out_stored, 16)
            sp.dma_start(out[(NB - 1) * P:N, :], agg[0:TAIL, NB - 1, :]).then_inc(out_stored, 16)
            sp.wait_ge(out_stored, 32)

        @block.gpsimd
        def _(pool):
            pool.memset(ident[:, :], 0.0).then_inc(pool_made, 1)
            pool.memset(before[:, :], 1.0).then_inc(pool_made, 1)
            pool.iota(iota_lo[:, :, :], pattern=[[1, P], [0, T]], base=0, channel_multiplier=0,
                      allow_small_or_imprecise_dtypes=True)
            pool.iota(iota_f[:, :], pattern=[[1, P]], base=0, channel_multiplier=0,
                      allow_small_or_imprecise_dtypes=True)
            pool.iota(slot_id[:, :], pattern=[[P, KT]], base=0, channel_multiplier=1,
                      allow_small_or_imprecise_dtypes=True)
            pool.iota(high_id[:, :], pattern=[[KT * P, NQ]], base=0, channel_multiplier=0,
                      allow_small_or_imprecise_dtypes=True)
            pool.iota(pow_i[:, :], pattern=[[0, 1]], base=127 + 63, channel_multiplier=-1)
            pool.wait_ge(pool_made, 2)
            pool.affine_select(out=ident[:, :], in_=ident[:, :], compare_op=ALU.not_equal, fill=1.0,
                               base=0, pattern=[[-1, P]], channel_multiplier=1)
            pool.affine_select(out=before[:, :], in_=before[:, :], compare_op=ALU.is_gt, fill=0.0,
                               base=0, pattern=[[1, P]], channel_multiplier=-1).then_inc(consts_ready, 1)

            def hold(semaphore, value):
                pool.wait_ge(semaphore, value)
                pool.sem_inc(pool_turn, 1)

            def gather(into, table, index):
                return pool.indirect_dma_start(out=into, out_offset=None, in_=table,
                                               in_offset=bass.IndirectOffsetOnAxis(index, 0))

            pool.wait_ge(table_stored[0], 16)
            pool.wait_ge(dram_cleared, 16 * (EP // CHUNK + COPIES))
            for h in range(NB):
                pool.indirect_dma_start(
                    out=xd_rows, out_offset=bass.IndirectOffsetOnAxis(start_i[:, h:h + 1], 0),
                    in_=node_tab[:, h, 1:R + 1], in_offset=None, bounds_check=E - 1, oob_is_err=False,
                ).then_inc(starts_put, 16)
            gather(first_tab[:, :], table0, first_i[:, :]).then_inc(first_row, 16)

            def gather_sources(k, j):
                for t in range(j * TD // BATCHES, (j + 1) * TD // BATCHES):
                    gather(xsd[:, k, t, 0:R], table0, idx[:, k, t:t + 1]).then_inc(gathered[0][k], 16)

            def scatter_messages(k, j):
                for t in range(j * BATCH, (j + 1) * BATCH):
                    pool.indirect_dma_start(
                        out=src_sums[t % COPIES], out_offset=bass.IndirectOffsetOnAxis(put_i[:, k, t:t + 1], 0),
                        in_=merged[:, k, t, :], in_offset=None, bounds_check=NPAD - 1, oob_is_err=False,
                        compute_op=ALU.add).then_inc(scattered[k], 16)

            LAG = SLOTS - 1

            def scatter_batch(i, b, j):
                if j == 0:
                    hold(merged_ready, i * SLOTS + (b + 2))
                    if b > 0:
                        hold(scattered[b - 1], i * (16 * T) + 16 * T)
                    elif not isinstance(i, int) or i > 0:
                        hold(scattered[SLOTS - 1], i * (16 * T))
                else:
                    hold(scattered[b], i * (16 * T) + 16 * BATCH * j)
                scatter_messages(b, j)

            for k in range(LAG):
                pool.wait_ge(idx_ready[0], k + 1)
                for j in range(BATCHES):
                    gather_sources(k, j)

            def gather_and_scatter(i, k, b_i, b):
                hold(idx_ready[0], i * SLOTS + (k + 1))
                for j in range(BATCHES):
                    gather_sources(k, j)
                    scatter_batch(b_i, b, j)

            gather_and_scatter(0, LAG, 0, 0)
            with pool.Fori(1, ITERS) as i:
                for k in range(LAG):
                    gather_and_scatter(i, k, i - 1, k + 1)
                gather_and_scatter(i, LAG, i, 0)
            gather_and_scatter(ITERS, 0, ITERS - 1, 1)
            for b_i, b in ((ITERS - 1, 2), (ITERS - 1, 3), (ITERS, 0)):
                for j in range(BATCHES):
                    scatter_batch(b_i, b, j)

            def gather_ends(l):
                for k in range(SLOTS):
                    pool.wait_ge(sums_stored[l][k], 16 * (ITERS + 1 + (k == 0)))
                for h in range(NB):
                    gather(agg[:, h, :], runsums[l], end_i[:, h:h + 1]).then_inc(ends_got[l], 16)

            gather_ends(0)
            for l in (1, 2):
                pool.wait_ge(table_stored[l], 16)

                def gather_rows(i, k):
                    hold(idx_ready[l], i * SLOTS + (k + 1))
                    for t in range(TD):
                        gather(rows[:, k, t, :], tables[l - 1], idx[:, k, t:t + 1]).then_inc(gathered[l][k], 16)

                with pool.Fori(0, ITERS) as i:
                    for k in range(SLOTS):
                        gather_rows(i, k)
                gather_rows(ITERS, 0)
                gather_ends(l)

        @block.scalar
        def _(act):
            act.wait_ge(weights_cleared, 1)
            w1_t = mlp_w1.rearrange("o f -> f o")
            w2_t = mlp_w2.rearrange("o f -> f o")
            n = 0
            for to, of in (
                (w1c[:, 0:HID], w1_t), (w1c[0:D, HID:P], w1_t[D:2 * D, :]), (w1c[D:2 * D, HID:P], w1_t[0:D, :]),
                (b1c[0:HID, :], mlp_b1.rearrange("(o a) -> o a", a=1)),
                (b1c[HID:P, :], mlp_b1.rearrange("(o a) -> o a", a=1)),
                (w2c[0:HID, 0:D], w2_t), (w2c[HID:P, D:2 * D], w2_t),
                (b2c[:, 0:D], mlp_b2.partition_broadcast(P)), (b2c[:, D:2 * D], mlp_b2.partition_broadcast(P)),
                (gcn_b[0][:, :], gcn_b1.partition_broadcast(P)), (gcn_b[1][:, :], gcn_b2.partition_broadcast(P)),
                *((gcn_w[l][b * D:(b + 1) * D, b * D:(b + 1) * D], w)
                  for l, w in enumerate((gcn_w1, gcn_w2)) for b in range(PER)),
            ):
                act.dma_start(to, of).then_inc(weights_loaded, 16)
                n += 1
            assert n == 11 + 2 * PER
            act.wait_ge(zeros_ready, 1)
            for c in range(0, EP, CHUNK):
                act.dma_start(xd_v[:, c:c + CHUNK, :], zeros.rearrange("p (t c) -> p t c", c=R)).then_inc(dram_cleared, 16)
            for c in range(COPIES):
                act.dma_start(src_sums[c].rearrange("(p h) c -> p (h c)", p=P), zeros[:, 0:NB * D]).then_inc(dram_cleared, 16)

            def root(n):
                act.wait_ge(sqrt_in, n)
                act.activation(st[1][:, :], st[0][:, :], ACT.Sqrt).then_inc(sqrt_out, 1)

            root(1)
            root(2)
            act.wait_ge(weights_loaded, 16 * (11 + 2 * PER))

            def copy_low(l, n):
                act.wait_ge(low_ready[l], n)
                act.activation(low_row[:, :], ps_low, ACT.Copy).then_inc(low_copied[l], 1)

            def turn(g, second, first):
                for j, cols in enumerate(PARTS):
                    w = len(cols) * P
                    act.wait_ge(xt_ready, g * SUBS + (j + 1))
                    act.activation(xt[:, 0:w], ps_xt[:, 0:w], ACT.Copy).then_inc(xt_copied, 1)
                    if j == 1 and second:
                        copy_low(0, g * QUADS + 2 * QUADS)
                    if j == SUBS - 1 and first:
                        copy_low(0, g * QUADS + (2 * QUADS + 1))
                    act.wait_ge(h_ready, g * SUBS + (j + 1))
                    act.activation(hid[:, 0:w], ps_h[:, 0:w], ACT.Relu, bias=b1c[:, :]).then_inc(h_done, 1)

            for n in range(QUADS + 1):
                copy_low(0, n + 1)
            with act.Fori(0, GROUPS - 2) as g:
                turn(g, True, True)
            turn(GROUPS - 2, True, False)
            turn(GROUPS - 1, False, False)
            root(3)
            for l in (1, 2):
                act.wait_ge(nt_ready, l)
                for c in range(0, NG * P, BANK):
                    e = min(c + BANK, NG * P)
                    last = act.activation(node_xt[:, c:e], ps_nt[:, c:e], ACT.Copy)
                last.then_inc(nt_copied, 1)
                with act.Fori(0, GROUPS * QUADS + 1) as n:
                    copy_low(l, n + 1)
                act.wait_ge(tanh_in, l)
                act.activation(node_h[:, 0:NB, :], agg[:, :, :], ACT.Tanh).then_inc(tanh_out, 1)
            root(4)

        @block.tensor
        def _(pe):
            pe.wait_ge(zeros_ready, 1)
            for e in range(2):
                nc.tensor.matmul(ps_cnt[e], zeros[:, 0:P], zeros[:, 0:NB], start=True, stop=False)
            with pe.Fori(0, GROUPS) as i:
                for e in range(2):
                    pe.wait_ge(hot_ready, i * 2 + (e + 1))
                    for t in range(T):
                        last = nc.tensor.matmul(ps_cnt[e], hot_lo[e][:, :, t], hot_hi[e][:, :, t], start=False, stop=False)
                    last.then_inc(hot_free, 1)
            for e in range(2):
                last = nc.tensor.matmul(ps_cnt[e], zeros[:, 0:P], zeros[:, 0:NB], start=False, stop=True)
            last.then_inc(counted, 1)
            pe.wait_ge(consts_ready, 1)
            pe.wait_ge(prefix_in, 1)
            nc.tensor.matmul(ps_pre, before[:, :], cnt[:, 1, :], start=True, stop=True)
            nc.tensor.matmul(ps_tot, ones[:, :], cnt[:, 1, :], start=True, stop=True).then_inc(prefix_out, 1)

            pe.wait_ge(weights_loaded, 16 * (11 + 2 * PER))

            def spread_low(l, k, q):
                for u in range(QUAD):
                    t = TD + q * QUAD + u
                    last = nc.tensor.matmul(ps_low[:, u * P:(u + 1) * P], low_s[:, k, t:t + 1].to_broadcast([P, P]),
                                            ident_h[:, :], start=True, stop=True)
                last.then_inc(low_ready[l], 1)

            def gather_column(l, w, u, bank):
                q, c0, at = u // QUAD, u % QUAD * P, u % 2 * NQ * w
                for c in range(KT):
                    for part in range(3):
                        last = nc.tensor.matmul(ps_pair[bank][:, at:at + NQ * w], hot[:, q, c, c0:c0 + P],
                                                parts[:, c, part, 0:NQ * w],
                                                start=c == part == 0, stop=c == KT - 1 and part == 2)
                if u % 2:
                    last.then_inc(pair_ready[l], 1)

            def count(i, k, per, more):
                return i * (SLOTS * per) + (k * per + more)

            def merge(i, k):
                pe.wait_ge(msgs_ready, count(i, k, 1, 1))
                for t in range(T):
                    for part in range(3):
                        w = R if part == 0 else D
                        last = nc.tensor.matmul(ps_mg[:, t, 0:w], same[:, k % 2, t, :], msg_parts[:, t, PW[part]:PW[part] + w],
                                                start=part == 0, stop=part == 2)
                last.then_inc(merge_ready, 1)

            def turn(i, k, merges=True, nexts=2):
                s = k % SLOTS
                columns = {0: (0,), 1: (1,), 2: (2,), 3: (3,), 4: (4, 5), 5: (6,), 6: (7,)}
                pe.wait_ge(gathered[0][s], (i + k // SLOTS) * (16 * TD) + 16 * TD)
                pe.wait_ge(picked[0], count(i, k, PAIRS, PAIRS))
                pe.wait_ge(xd_spread, count(i, k, 1, 1))
                def reflections(j):
                    pe.wait_ge(h_done, count(i, k, SUBS, j + 1))
                    if j == 0:
                        pe.wait_ge(v_free, count(i, k, 1, 1))
                    for u, t in enumerate(PARTS[j]):
                        last = nc.tensor.matmul(ps_v[:, t, :], hid[:, u * P:(u + 1) * P], w2c[:, :], start=True, stop=True)
                    if j == SUBS - 1:
                        last.then_inc(v_ready, 1)

                for j, cols in enumerate(PARTS):
                    for u, t in enumerate(cols):
                        last = nc.tensor.transpose(ps_xt[:, u * P:(u + 1) * P], xsd[:, s, t, 1:1 + 2 * D], ident[:, :])
                    last.then_inc(xt_ready, 1)
                    if nexts > 0:
                        for u in columns[j]:
                            if u % QUAD == 0:
                                pe.wait_ge(slot_hot[0], count(i, k, QUADS, QUADS + u // QUAD + 1))
                            if u % 2 == 0:
                                pe.wait_ge(pair_free[0], count(i, k, PAIRS, PAIRS + u // 2 + 1))
                            gather_column(0, R, u, u // 2 % BANKS)
                        if j == 1:
                            if merges:
                                pe.wait_ge(merged_ready, count(i, k, 1, 0))
                            spread_low(0, (k + 1) % SLOTS, 1)
                    if j == SUBS - 1 and nexts > 1:
                        pe.wait_ge(idx_ready[0], count(i, k, 1, 3))
                        spread_low(0, (k + 2) % SLOTS, 0)
                    if j > 0:
                        reflections(j - 1)
                        pe.wait_ge(same_ready, count(i, k, SUBS, j))
                    for u, t in enumerate(cols):
                        for add, of in enumerate((low_s, high_s)):
                            last = nc.tensor.matmul(ps_eq[:, u, :], of[:, s, t:t + 1].to_broadcast([P, P]), ident_h[:, :],
                                                    start=add == 0, stop=add == 1)
                    last.then_inc(row_ready, 1)
                    pe.wait_ge(xt_copied, count(i, k, SUBS, j + 1))
                    w = len(cols) * P
                    nc.tensor.matmul(ps_h[:, 0:w], w1c[:, :], xt[:, 0:w], start=True, stop=True).then_inc(h_ready, 1)
                reflections(SUBS - 1)
                pe.wait_ge(same_ready, count(i, k, SUBS, SUBS))
                if merges:
                    if nexts > 1:
                        pe.wait_ge(low_copied[0], count(i, k, QUADS, 2 * QUADS + 1))
                    else:
                        pe.wait_ge(low_copied[0], GROUPS * QUADS)
                    merge(i, k - 1)

            pe.wait_ge(parts_ready[0], 1)
            pe.wait_ge(idx_ready[0], SLOTS)
            spread_low(0, 0, 0)
            for u in range(TP):
                if u % QUAD == 0:
                    pe.wait_ge(slot_hot[0], u // QUAD + 1)
                    if u == 0:
                        spread_low(0, 0, 1)
                    else:
                        spread_low(0, 1, 0)
                if u % 2 == 0:
                    pe.wait_ge(pair_free[0], u // 2 + 1)
                gather_column(0, R, u, u // 2 % BANKS)
            turn(0, 0, merges=False)
            with pe.Fori(0, ITERS - 1) as i:
                for k in range(1, SLOTS + 1):
                    turn(i, k)
            for g in range((ITERS - 1) * SLOTS + 1, GROUPS):
                turn(ITERS - 1, g - (ITERS - 1) * SLOTS, nexts=GROUPS - 1 - g)
            merge(ITERS, 0)

            def spans(l):
                pe.wait_ge(span_in[l], 1)
                flat = tmp[:, :, :].rearrange("p h c -> p (h c)")
                for c in range(0, NB * D, BANK):
                    e = min(c + BANK, NB * D)
                    last = nc.tensor.matmul(ps_span[:, c:e], last_lo[:, :], flat[:, c:e], start=True, stop=True)
                last.then_inc(span_out[l], 1)

            spans(0)
            for l in (1, 2):
                pe.wait_ge(nt_in, l)
                flat = node_h[:, :, :].rearrange("p h c -> p (h c)")
                for b in range(NG):
                    last = nc.tensor.transpose(ps_nt[:, b * P:(b + 1) * P], flat[:, b * P:(b + 1) * P], ident[:, :])
                last.then_inc(nt_ready, 1)
                pe.wait_ge(nt_copied, l)
                for b in range(NG):
                    last = nc.tensor.matmul(ps_nh[:, b * P:(b + 1) * P], node_xt[:, b * P:(b + 1) * P], gcn_w[l - 1][:, :],
                                            start=True, stop=True)
                last.then_inc(nh_ready, 1)

                def gather_group(i, k):
                    for q in range(QUADS):
                        pe.wait_ge(slot_hot[l], count(i, k, QUADS, q + 1))
                        if q == QUADS - 1:
                            pe.wait_ge(idx_ready[l], count(i, k, 1, 2))
                            spread_low(l, (k + 1) % SLOTS, 0)
                        else:
                            spread_low(l, k, q + 1)
                        for u in range(q * QUAD, (q + 1) * QUAD):
                            if u % 2 == 0:
                                pe.wait_ge(pair_free[l], count(i, k, PAIRS, u // 2 + 1))
                            gather_column(l, D, u, u // 2 % BANKS)

                pe.wait_ge(parts_ready[l], 1)
                pe.wait_ge(idx_ready[l], SLOTS)
                spread_low(l, 0, 0)
                with pe.Fori(0, ITERS) as i:
                    for k in range(SLOTS):
                        gather_group(i, k)
                gather_group(ITERS, 0)
                pe.wait_ge(low_copied[l], GROUPS * QUADS + 1)
                spans(l)

        @block.vector
        def _(dve):
            v = nc.vector
            done = [0]
            base = [0]

            def step(ins):
                done[0] += 1
                ins.then_inc(dve_done, 1)
                dve.wait_ge(dve_done, base[0] + done[0])

            v.memset(prev_last[:, :], -1)
            v.memset(src_i[:, EP:], 0)
            v.memset(keep[:, EP:], 0.0)
            v.memset(low_h[:, EP:], 0.0)
            v.memset(high_h[:, EP:], 0.0)
            v.memset(next_first[:, :], -1).then_inc(edges_cleared, 1)
            v.memset(gcn_w[0][:, :], 0.0)
            v.memset(gcn_w[1][:, :], 0.0)
            v.memset(w2c[:, :], 0.0).then_inc(weights_cleared, 1)
            v.memset(node_x[:, :, :], 0.0).then_inc(node_cleared, 1)
            v.memset(zeros, 0.0).then_inc(zeros_ready, 1)
            v.memset(ones[:, :], 1.0)
            v.memset(node_tab[:, :, :], 0.0)
            step(v.memset(node_h[:, :, :], 0.0))
            dve.wait_ge(consts_ready, 1)
            v.tensor_copy(ident_h[:, :], ident[:, :])
            step(v.tensor_scalar(pow2_i[:, :], pow_i[:, :], 23, None, ALU.logical_shift_left))
            step(v.tensor_scalar(lead_max[:, :], pow2, 2.0, None, ALU.mult))

            dve.wait_ge(edges_loaded, 16 * 4)
            for e, ends in enumerate((src_i[:, 0:EP], dst_i)):
                step(v.tensor_scalar(split_i, ends, P - 1, None, ALU.bitwise_and))
                step(v.tensor_copy(lohi[e][0], split_i))
                step(v.tensor_scalar(split_i, ends, P.bit_length() - 1, None, ALU.arith_shift_right))
                step(v.tensor_copy(lohi[e][1], split_i))
            v.tensor_tensor(keep[:, 1:EP], dst_i[:, 1:EP], dst_i[:, 0:EP - 1], ALU.is_equal)
            v.tensor_tensor(keep[:, 0:1], dst_i[:, 0:1], prev_last[:, :], ALU.is_equal)
            v.tensor_tensor(runs_on[:, :], dst_i[:, EP - 1:EP], next_first[:, :], ALU.is_equal)
            v.tensor_copy(first_i[:, :], dst_i[:, 0:1])
            v.tensor_scalar(last_lohi_i[:, 0:1], dst_i[:, EP - 1:EP], P - 1, None, ALU.bitwise_and)
            step(v.tensor_scalar(last_lohi_i[:, 1:2], dst_i[:, EP - 1:EP], P.bit_length() - 1, None, ALU.arith_shift_right))
            step(v.tensor_copy(last_lohi[:, :], last_lohi_i[:, :]))
            v.tensor_scalar(last_lo[:, :], iota_f[:, :], last_lohi[:, 0:1], None, ALU.is_equal)
            step(v.tensor_scalar(last_hi[:, :], iota_f[:, 0:NB], last_lohi[:, 1:2], None, ALU.is_equal))

            def one_hots(e, col):
                lo = lohi[e][0][:, bass.ds(col, T)].unsqueeze(1)
                hi = lohi[e][1][:, bass.ds(col, T)].unsqueeze(1)
                v.tensor_tensor(hot_lo[e], lo.to_broadcast([P, P, T]), iota_lo, ALU.is_equal)
                v.tensor_tensor(hot_hi[e], hi.to_broadcast([P, NB, T]), iota_lo[:, 0:NB, :], ALU.is_equal).then_inc(hot_ready, 1)

            for e in range(2):
                one_hots(e, 0)
            with dve.Fori(1, GROUPS) as i:
                for e in range(2):
                    dve.wait_ge(hot_free, i * 2 + (e - 1))
                    one_hots(e, i * T)
            dve.wait_ge(counted, 1)
            for e in range(2):
                last = v.tensor_copy(cnt[:, e, :], ps_cnt[e])
            step(last)

            def rsqrt(n, to, arg):
                dve.wait_ge(sqrt_out, n)
                step(v.reciprocal(st[2][:, :], st[1][:, :]))
                step(v.tensor_tensor(st[3][:, :], st[2][:, :], st[2][:, :], ALU.mult))
                step(v.tensor_tensor(st[3][:, :], st[3][:, :], arg, ALU.mult))
                step(v.tensor_scalar(st[3][:, :], st[3][:, :], -0.5, 1.5, ALU.mult, ALU.add))
                step(v.tensor_tensor(to, st[2][:, :], st[3][:, :], ALU.mult))

            step(v.tensor_tensor(st[0][:, :], cnt[:, 0, :], cnt[:, 1, :], ALU.add))
            v.tensor_scalar(st[0][:, :], st[0][:, :], DEG_MIN, None, ALU.max).then_inc(sqrt_in, 1)
            dve.wait_ge(sqrt_in, 1)
            rsqrt(1, dis[:, :], st[0][:, :])
            v.tensor_scalar(st[0][:, :], cnt[:, 1, :], 1.0, None, ALU.add).then_inc(sqrt_in, 1)
            dve.wait_ge(sqrt_in, 2)
            rsqrt(2, dinv[:, :], st[0][:, :])
            v.tensor_scalar(has_in[:, :], cnt[:, 1, :], 0.0, None, ALU.is_gt).then_inc(prefix_in, 1)
            dve.wait_ge(prefix_out, 1)
            step(v.tensor_copy(st[0][:, :], ps_tot))
            step(v.tensor_tensor_scan(total[:, :], ones[:, 0:NB], st[0][:, :], 0.0, ALU.mult, ALU.add))
            step(v.tensor_tensor(total[:, :], total[:, :], st[0][:, :], ALU.subtract))
            step(v.tensor_tensor(start[:, :], ps_pre, total[:, :], ALU.add))
            step(v.tensor_tensor(st[0][:, :], start[:, :], cnt[:, 1, :], ALU.add))
            step(v.tensor_scalar(end_i[:, :], st[0][:, :], -1.0, 0.0, ALU.add, ALU.max))
            dve.wait_ge(prefix_in, 1)
            step(v.tensor_scalar(st[1][:, :], has_in[:, :], -float(FAR), float(FAR), ALU.mult, ALU.add))
            step(v.tensor_tensor(start_i[:, :], st[1][:, :], start[:, :], ALU.add))
            dve.wait_ge(node_loaded, 32)
            v.tensor_copy(node_tab[:, 0:NB, 1:R], node_x[:, 0:NB, :])
            v.tensor_copy(node_tab[:, 0:NB, R:R + 1], dis[:, :].unsqueeze(2))
            v.tensor_copy(node_tab[:, 0:NB, 0:1], dis[:, :].unsqueeze(2)).then_inc(table_ready[0], 1)
            step(v.tensor_scalar(split_i, src_i[:, 0:EP], KT * P - 1, None, ALU.bitwise_and))
            step(v.tensor_copy(low_h[:, 0:EP], split_i))
            step(v.tensor_tensor(high_h[:, 0:EP], src_i[:, 0:EP], split_i, ALU.subtract))

            def split_table(l, table, w):
                rest = wide_tmp[:, 0:NBP * w].rearrange("p (h c) -> p h c", c=w)
                by = "p (b k) c -> p k b c"
                left = table
                for part in range(3):
                    piece = parts[:, :, part, 0:NQ * w].rearrange("p k (b c) -> p k b c", c=w)
                    if part < 2:
                        step(v.tensor_copy(piece, left.rearrange(by, k=KT)))
                        step(v.tensor_tensor(rest.rearrange(by, k=KT), left.rearrange(by, k=KT), piece, ALU.subtract))
                        left = rest
                    else:
                        v.tensor_copy(piece, left.rearrange(by, k=KT)).then_inc(parts_ready[l], 1)
                dve.wait_ge(parts_ready[l], 1)

            def stage(l, k, col):
                if l == 0:
                    v.tensor_copy(src_f[:, k, :], src_i[:, bass.ds(col, T)])
                v.tensor_copy(keep_s[:, k, :], keep[:, bass.ds(col, T)])
                v.tensor_copy(low_s[:, k, :], low_h[:, bass.ds(col, T)])
                step(v.tensor_copy(high_s[:, k, :], high_h[:, bass.ds(col, T)]))
                v.tensor_tensor(high_hot[:, k, :, :], high_s[:, k, TD:].unsqueeze(2).to_broadcast([P, TP, NQ]),
                                high_id[:, :].unsqueeze(1).to_broadcast([P, TP, NQ]), ALU.is_equal)
                v.tensor_copy(idx[:, k, :], src_i[:, bass.ds(col, T)]).then_inc(idx_ready[l], 1)

            def count(i, k, per, more):
                return i * (SLOTS * per) + (k * per + more)

            def hot_rows(l, i, k, q):
                dve.wait_ge(low_copied[l], count(i, k, QUADS, q + 1))
                for c in range(KT):
                    last = v.tensor_scalar(hot[:, q, c, :], low_row[:, :], slot_id[:, c:c + 1], None, ALU.is_equal)
                last.then_inc(slot_hot[l], 1)

            def pick(l, w, i, k, pair, bank, to):
                s = k % SLOTS
                prods = picked_sb[:, 0:2 * NQ * w].rearrange("p (t b c) -> p t b c", t=2, c=w)
                dve.wait_ge(pair_ready[l], count(i, k, PAIRS, pair + 1))
                v.tensor_tensor(prods, ps_pair[bank][:, 0:2 * NQ * w].rearrange("p (t b c) -> p t b c", t=2, c=w),
                                high_hot[:, s, 2 * pair:2 * pair + 2, :].unsqueeze(3).to_broadcast([P, 2, NQ, w]),
                                ALU.mult).then_inc(pair_free[l], 1)
                dve.wait_ge(pair_free[l], count(i, k, PAIRS, pair + 1 + BANKS))
                v.tensor_reduce(to, prods.rearrange("p t b c -> p t c b"), AX.X, ALU.add).then_inc(picked[l], 1)
                dve.wait_ge(picked[l], count(i, k, PAIRS, pair + 1))

            def running_sums(l, i, k, values):
                s = k % SLOTS
                dve.wait_ge(sums_stored[l][s], (i + k // SLOTS) * 16 + 16)
                for c in range(D):
                    last = v.tensor_tensor_scan(sums[:, s, :, c], keep_s[:, s, :], values(c),
                                                sums[:, (s - 1) % SLOTS, T - 1, c:c + 1], ALU.mult, ALU.add)
                last.then_inc(sums_ready[l], 1)
                dve.wait_ge(sums_ready[l], count(i, k, 1, 1))

            def start_pass(l):
                step(v.memset(sums[:, SLOTS - 1, T - 1, :], 0.0))
                for k in range(SLOTS):
                    stage(l, k, k * T)
                dve.wait_ge(idx_ready[l], SLOTS)
                dve.sem_inc(pair_free[l], BANKS)

            split_table(0, node_tab[:, :, 0:R], R)
            step(v.tensor_copy(msg_parts[:, :, D], pow2.to_broadcast([P, T])))
            dve.sem_inc(v_free, 1)
            dve.sem_inc(merged_ready, 1)
            start_pass(0)
            dve.wait_ge(weights_loaded, 16 * (11 + 2 * PER))
            dve.wait_ge(first_row, 16)
            v.tensor_copy(xsd[:, SLOTS - 1, T - 1, R:R + D], first_tab[:, 1:R])
            step(v.tensor_copy(xsd[:, SLOTS - 1, T - 1, R + D:2 * R], first_tab[:, 0:1]))

            def spread_rows(i, k):
                s = k % SLOTS
                dve.wait_ge(xd_loaded[s], (i + k // SLOTS) * 16 + 16)
                for c in range(R):
                    last = v.tensor_tensor_scan(xsd[:, s, :, R + c], keep_s[:, s, :], xd_in[:, s, :, c],
                                                xsd[:, (s - 1) % SLOTS, T - 1, R + c:R + c + 1], ALU.mult, ALU.add)
                last.then_inc(xd_spread, 1)
                dve.wait_ge(xd_spread, count(i, k, 1, 1))

            def equal_sources(i, k, j):
                s, part = k % SLOTS, PARTS[j]
                cols, w = slice(part.start, part.stop), len(part)
                dve.wait_ge(row_ready, count(i, k, SUBS, j + 1))
                v.tensor_tensor(same[:, k % 2, cols, :], ps_eq[:, 0:w, :],
                                src_f[:, s, cols].unsqueeze(2).to_broadcast([P, w, P]), ALU.is_equal).then_inc(same_ready, 1)

            def pick_rows(i, k, pair):
                t = TD + 2 * pair
                pick(0, R, i, k, pair, pair % BANKS, xsd[:, k % SLOTS, t:t + 2, 0:R])

            def turn(i, k, nexts=3):
                g1 = count(i, k, 1, 1)
                wide = [P, T, 2, D]

                def equal(j):
                    if nexts > 0:
                        equal_sources(i, k + 1, j)

                def hot(q):
                    if nexts > 1:
                        hot_rows(0, i, k + 2, q)

                def pick(pair):
                    if nexts > 1:
                        pick_rows(i, k + 2, pair)

                dve.wait_ge(v_ready, g1)
                v.tensor_tensor(refl.rearrange("p t s c -> p t (s c)"), ps_v,
                                b2c[:, :].unsqueeze(1).to_broadcast([P, T, 2 * D]), ALU.add).then_inc(v_free, 1)
                dve.wait_ge(v_free, count(i, k, 1, 2))
                step(v.tensor_tensor(prod, refl, refl, ALU.mult))
                equal(0)
                if nexts > 1:
                    spread_rows(i, k + 2)
                step(v.tensor_reduce(scale2, prod, AX.X, ALU.add))
                step(v.tensor_scalar(scale2, scale2, NORM_MIN, 0.5, ALU.max, ALU.mult))
                equal(1)
                step(v.reciprocal(scale2, scale2))
                step(v.tensor_tensor(xw, xsd[:, k % SLOTS, :, 1:1 + 2 * D].rearrange("p t (s c) -> p t s c", s=2),
                                     xsd[:, k % SLOTS, :, 0:2 * R:2 * R - 1].unsqueeze(3).to_broadcast(wide), ALU.mult))
                equal(2)
                pick(0)
                hot(1)
                step(v.tensor_tensor(prod, refl, xw, ALU.mult))
                step(v.tensor_reduce(dots, prod, AX.X, ALU.add))
                step(v.tensor_tensor(dots, dots, scale2, ALU.mult))
                step(v.tensor_tensor(prod, refl, dots.unsqueeze(3).to_broadcast(wide), ALU.mult))
                equal(3)
                step(v.tensor_tensor(mirrored, xw, prod, ALU.subtract))
                pick(1)
                for s in range(2):
                    last = v.tensor_tensor(prod[:, :, s, :], refl[:, :, s, :], mirrored[:, :, 1 - s, :], ALU.mult)
                step(last)
                equal(4)
                step(v.tensor_reduce(dots, prod, AX.X, ALU.add))
                step(v.tensor_tensor(dots, dots, scale2, ALU.mult))
                step(v.tensor_tensor(prod, refl, dots.unsqueeze(3).to_broadcast(wide), ALU.mult))
                equal(5)
                for s in range(2):
                    last = v.tensor_tensor(msgs[:, :, s, :], mirrored[:, :, 1 - s, :], prod[:, :, s, :], ALU.subtract)
                step(last)
                left = msgs[:, :, 0, :]
                for part in range(3):
                    piece = msg_parts[:, :, PW[part]:PW[part] + D]
                    if part < 2:
                        step(v.tensor_copy(piece, left))
                        step(v.tensor_tensor(prod[:, :, 0, :], left, piece, ALU.subtract))
                        left = prod[:, :, 0, :]
                    else:
                        v.tensor_copy(piece, left).then_inc(msgs_ready, 1)
                pick(2)
                running_sums(0, i, k, lambda c: msgs[:, :, 1, c])
                equal(6)
                pick(3)
                if nexts > 2:
                    hot_rows(0, i, k + 3, 0)
                dve.wait_ge(merge_ready, g1)
                step(v.tensor_scalar(late, ps_mg[:, :, D], lead_max[:, :], float(SKIP), ALU.is_gt, ALU.mult))
                step(v.tensor_tensor(put_i[:, k % SLOTS, :], late, src_f[:, k % SLOTS, :], ALU.add))
                v.tensor_copy(merged[:, k % SLOTS, :, :], ps_mg[:, :, 0:D]).then_inc(merged_ready, 1)
                stage(0, k % SLOTS, i * STEP + (STEP + k * T))

            spread_rows(0, 0)
            spread_rows(0, 1)
            for q in range(QUADS):
                hot_rows(0, 0, 0, q)
                pick_rows(0, 0, 2 * q)
                pick_rows(0, 0, 2 * q + 1)
            hot_rows(0, 0, 1, 0)
            for j in range(SUBS):
                equal_sources(0, 0, j)
                if j in (1, 3, 4, 6):
                    pick_rows(0, 1, (1, 3, 4, 6).index(j))
                if j == 2:
                    hot_rows(0, 0, 1, 1)
            hot_rows(0, 0, 2, 0)
            LINKS = 22
            before_loop = done[0]
            with dve.Fori(0, ITERS - 1) as i:
                done[0], base[0] = 0, i * (LINKS * SLOTS) + before_loop
                for k in range(SLOTS):
                    turn(i, k)
                assert done[0] == LINKS * SLOTS, done[0]
            base[0], done[0] = 0, before_loop + (ITERS - 1) * LINKS * SLOTS
            for g in range((ITERS - 1) * SLOTS, GROUPS):
                turn(ITERS - 1, g - (ITERS - 1) * SLOTS, nexts=GROUPS - 1 - g)

            def node_sums(l):
                step(v.tensor_scalar(last_row[:, :], sums[:, (GROUPS - 1) % SLOTS, T - 1, :], runs_on[:, :], None, ALU.mult))
                v.tensor_tensor(tmp[:, :, :], last_hi[:, :].unsqueeze(2).to_broadcast([P, NB, D]),
                                last_row[:, :].unsqueeze(1).to_broadcast([P, NB, D]), ALU.mult).then_inc(span_in[l], 1)
                dve.wait_ge(ends_got[l], 16 * NB)
                step(v.tensor_tensor(agg[:, :, :], agg[:, :, :], has_in[:, :].unsqueeze(2).to_broadcast([P, NB, D]), ALU.mult))
                dve.wait_ge(span_out[l], 1)
                step(v.tensor_tensor(agg[:, :, :], agg[:, :, :], ps_span.rearrange("p (h c) -> p h c", c=D), ALU.add))

            def per_node(a):
                return a[:, :].unsqueeze(2).to_broadcast([P, NB, D])

            def layernorm(n, to, a):
                step(v.tensor_reduce(st[0][:, :], a, AX.X, ALU.add))
                step(v.tensor_scalar(st[0][:, :], st[0][:, :], 1.0 / D, None, ALU.mult))
                step(v.tensor_tensor(a, a, per_node(st[0]), ALU.subtract))
                step(v.tensor_tensor(tmp[:, :, :], a, a, ALU.mult))
                step(v.tensor_reduce(st[0][:, :], tmp[:, :, :], AX.X, ALU.add))
                v.tensor_scalar(st[0][:, :], st[0][:, :], 1.0 / D, LN_EPS, ALU.mult, ALU.add).then_inc(sqrt_in, 1)
                dve.wait_ge(sqrt_in, n)
                rsqrt(n, st[3][:, :], st[0][:, :])
                return v.tensor_tensor(to, a, per_node(st[3]), ALU.mult)

            node_sums(0)
            dve.wait_ge(acc_loaded, 16 * COPIES)
            for c in range(COPIES):
                step(v.tensor_tensor(agg[:, :, :], agg[:, :, :], acc_in[c], ALU.add))
            step(v.tensor_tensor(agg[:, :, :], agg[:, :, :], per_node(dis), ALU.mult))
            step(v.tensor_tensor(agg[:, :, :], agg[:, :, :], node_x[:, 0:NB, :], ALU.add))
            step(v.tensor_scalar(agg[:, :, :], agg[:, :, :], 0.0, None, ALU.max))
            step(v.tensor_tensor(agg[:, :, :], agg[:, :, :], node_x[:, 0:NB, :], ALU.add))
            step(layernorm(3, node_h[:, 0:NB, :], agg[:, :, :]))
            v.tensor_copy(node_x[:, 0:NB, :], node_h[:, 0:NB, :]).then_inc(nt_in, 1)

            for l in (1, 2):
                dve.wait_ge(nh_ready, l)
                step(v.tensor_tensor(node_t[:, 0:NB, :], ps_nh[:, 0:NB * D].rearrange("p (h c) -> p h c", c=D),
                                     per_node(dinv), ALU.mult))
                v.memset(node_t[:, NB:, :], 0.0).then_inc(table_ready[l], 1)
                dve.wait_ge(table_ready[l], 1)
                split_table(l, node_t, D)
                for k in range(SLOTS):
                    dve.wait_ge(sums_stored[l - 1][k], 16 * (ITERS + 1 + (k == 0)))
                start_pass(l)

                def turn(i, k):
                    to = rows[:, k, TD:, :]
                    pick(l, D, i, k, 0, 0, to[:, 0:2, :])
                    hot_rows(l, i, k, 1)
                    pick(l, D, i, k, 1, 1, to[:, 2:4, :])
                    pick(l, D, i, k, 2, 0, to[:, 4:6, :])
                    hot_rows(l, i, k + 1, 0)
                    pick(l, D, i, k, 3, 1, to[:, 6:8, :])
                    dve.wait_ge(gathered[l][k], i * (16 * TD) + 16 * TD)
                    running_sums(l, i, k, lambda c: rows[:, k, :, c])
                    stage(l, k, i * STEP + (STEP + k * T))

                hot_rows(l, 0, 0, 0)
                before_loop = done[0]
                with dve.Fori(0, ITERS) as i:
                    done[0], base[0] = 0, i * SLOTS + before_loop
                    for k in range(SLOTS):
                        turn(i, k)
                    assert done[0] == SLOTS
                base[0], done[0] = 0, before_loop + ITERS * SLOTS
                turn(ITERS, 0)
                node_sums(l)
                step(v.tensor_tensor(agg[:, :, :], agg[:, :, :], node_t[:, 0:NB, :], ALU.add))
                step(v.tensor_tensor(agg[:, :, :], agg[:, :, :], per_node(dinv), ALU.mult))
                v.tensor_tensor(agg[:, :, :], agg[:, :, :], gcn_b[l - 1][:, :].unsqueeze(1).to_broadcast([P, NB, D]),
                                ALU.add).then_inc(tanh_in, 1)
                dve.wait_ge(tanh_out, l)
                if l == 1:
                    dve.drain().then_inc(nt_in, 1)
            step(v.tensor_tensor(node_x[:, 0:NB, :], node_x[:, 0:NB, :], node_h[:, 0:NB, :], ALU.add))
            layernorm(4, agg[:, :, :], node_x[:, 0:NB, :]).then_inc(out_ready, 1)


_INS = ['x', 'src', 'dst', 'L0_gnn_W1', 'L0_gnn_b1', 'L0_gnn_W2', 'L0_gnn_b2',
        'L1_gnn_W1', 'L1_gnn_b1', 'L1_gnn_W2', 'L1_gnn_b2']


def kernel(**inputs):
    import numpy as _np
    import concourse.bacc as _bacc
    from concourse import mybir as _mybir
    from concourse.bass_utils import run_bass_kernel_spmd as _run

    nc = _bacc.Bacc("TRN2", target_bir_lowering=False, num_devices=1)
    arrays, args = {}, []
    for name in _INS:
        a = _np.ascontiguousarray(inputs[name])
        arrays[f"in_{name}_dram"] = a
        args.append(nc.dram_tensor(f"in_{name}_dram", a.shape, _mybir.dt.from_np(a.dtype), kind="ExternalInput").ap())
    args.append(nc.dram_tensor("out_0_dram", inputs["x"].shape, _mybir.dt.float32, kind="ExternalOutput").ap())
    gnn_kernel(nc, *args)
    r = _run(nc, [arrays], core_ids=[0])
    return r.results[0]["out_0_dram"]
```

```python
import math
import numpy as np
import concourse.bass as bass
import concourse.mybir as mybir
from contextlib import ExitStack


def ceil_div(a, b):
    return -(-a // b)


def gnn_kernel(nc, x, src, dst, mlp_w1, mlp_b1, mlp_w2, mlp_b2, gcn_w1, gcn_b1, gcn_w2, gcn_b2, out):
    F32, I32, BF16, F16 = mybir.dt.float32, mybir.dt.int32, mybir.dt.bfloat16, mybir.dt.float16
    ALU, ACT, AX = mybir.AluOpType, mybir.ActivationFunctionType, mybir.AxisListType

    P = 128
    N, D = x.shape
    E = src.shape[0]
    HID = mlp_w1.shape[0]
    EP = E // P
    T = 25
    GROUPS = EP // T
    SLOTS = 4
    STEP = T * SLOTS
    ITERS = GROUPS // SLOTS
    TP = 8
    TD = T - TP
    TS = 7
    TH = T - TS
    BLOCK = math.isqrt(EP - 1) + 1
    BLOCKS = ceil_div(EP, BLOCK)
    EPAD = BLOCK * BLOCKS
    QUAD, QUADS, PAIRS = 4, TP // 4, TP // 2
    CHUNK = EP // 25
    assert EP * P == E and GROUPS * T == EP and ITERS * SLOTS + 1 == GROUPS
    assert 2 * HID == P and 2 * D == 32 and EP % 25 == 0
    BANKS = 2
    BATCH = 5
    BATCHES = T // BATCH
    BANK = 512
    SUBS = ceil_div(T, BANK // P)
    PARTS = [range(j * T // SUBS, (j + 1) * T // SUBS) for j in range(SUBS)]
    assert all(len(c) * P <= BANK for c in PARTS)
    NB = ceil_div(N, P)
    PER = P // D
    NG = ceil_div(NB, PER)
    NBP = NG * PER
    HB = NB // 2
    PROBES = 4
    assert NB % 2 == 0 and GROUPS % 2 == 1
    NPAD = NB * P
    TAIL = N - (NB - 1) * P
    KT = PER
    NQ = NBP // KT
    R = D + 1
    COPIES = BATCH
    SKIP = 1 << 14
    FAR = 1 << 20
    assert SKIP >= NPAD and FAR >= E
    LN_EPS, DEG_MIN, NORM_MIN = 1e-5, 1e-5, 1e-24

    ctx = ExitStack()
    with ctx:
        ctx.enter_context(nc.allow_non_contiguous_dma(reason="small transposed weights"))

        def sb(name, shape, dt=F32):
            return ctx.enter_context(nc.sbuf_tensor(name, shape, dt))

        def sem(name):
            return ctx.enter_context(nc.semaphore(name))

        def sems(name):
            return [sem(f"{name}{k}") for k in range(SLOTS)]

        def dram(name, shape):
            return nc.dram_tensor(name, shape, F32, kind="Internal").ap()

        table0 = dram("table0", [NPAD, R])
        tables = [dram(f"table{l}", [NPAD, D]) for l in (1, 2)]
        dst_samples = dram("dst_samples", [P, BLOCKS])
        dst_blocks = dram("dst_blocks", [P * BLOCKS, BLOCK])
        xd_rows = dram("xd_rows", [E, R])
        runsums = [dram(f"runsum{l}", [E, D]) for l in range(3)]
        src_sums = [dram(f"src_sum{c}", [NPAD, D]) for c in range(COPIES)]

        src_i = sb("src_i", [P, EP + STEP], I32)
        low_h = sb("low_h", [P, EP + STEP], F16)
        high_h = sb("high_h", [P, EP + STEP], F16)
        keep = sb("keep", [P, EP + STEP], BF16)
        prev_last = sb("prev_last", [P, 1], I32)
        next_first = sb("next_first", [P, 1], I32)
        first_i = sb("first_i", [P, 1], I32)
        first_lohi_i = sb("first_lohi_i", [P, 2], I32)
        first_lohi = sb("first_lohi", [P, 2])
        last_lohi_i = sb("last_lohi_i", [P, 2], I32)
        last_lohi = sb("last_lohi", [P, 2])
        runs_on = sb("runs_on", [P, 1])
        HOT_WORDS = QUADS * KT * QUAD * P // 2
        early = sb("early", [P, HOT_WORDS])
        hot = early[:, :].bitcast(BF16).rearrange("p (q c e) -> p q c e", q=QUADS, c=KT)
        zeros = early[:, 0:CHUNK * R]
        iota_lo = early[:, CHUNK * R + 1:CHUNK * R + 1 + P * T // 2].bitcast(BF16).rearrange("p (j t) -> p j t", t=T)
        assert CHUNK * R + 1 + P * T // 2 <= HOT_WORDS
        step_at = [sb(f"step_at{e}", [P, TS]) for e in range(2)]
        differ = sb("differ", [P, P])
        low_row = sb("low_row", [P, QUAD * P], F16)
        parts = sb("parts", [P, KT, 3, NQ * R], BF16)
        picked_sb = sb("picked_sb", [P, 2 * NQ * R])
        ident_h = sb("ident_h", [P, P], F16)
        slot_id = sb("slot_id", [P, KT])
        high_id = sb("high_id", [P, NQ], F16)
        iota_f = sb("iota_f", [P, P])
        ident = sb("ident", [P, P])
        follow = sb("follow", [P, P])
        wrap = sb("wrap", [P, P])
        node_id = sb("node_id", [P, NB])
        ones = sb("ones", [P, P])
        pow_i = sb("pow_i", [P, 1], I32)
        pow2_i = sb("pow2_i", [P, 1], I32)
        pow2 = pow2_i[:, :].bitcast(F32)
        lead_max = sb("lead_max", [P, 1])
        w1c = sb("w1c", [2 * D, P])
        b1c = sb("b1c", [P, 1])
        w2c = sb("w2c", [P, 2 * D])
        b2c = sb("b2c", [P, 2 * D])
        gcn_w = [sb(f"gcn_w{l}", [P, P]) for l in (1, 2)]
        gcn_b = [sb(f"gcn_b{l}", [P, D]) for l in (1, 2)]

        WORDS = 2 * EP + T * P + T * NB + 64
        shared = sb("shared", [P, WORDS])
        half = shared[:, :].bitcast(BF16)
        src_lohi = [half[:, h * EP:(h + 1) * EP] for h in range(2)]
        dst_f = shared[:, EP:EP + EPAD]
        hot_at = 2 * (EP + EPAD)
        assert EP + EPAD + T * (P + NB) <= WORDS
        hot_lo = [half[:, hot_at + e * P * T:hot_at + e * P * T + P * TH].rearrange("p (j t) -> p j t", t=TH)
                  for e in range(2)]
        step_lo = [half[:, hot_at + e * P * T + P * TH:hot_at + (e + 1) * P * T].rearrange("p (t j) -> p t j", j=P)
                   for e in range(2)]
        hot_at += 2 * P * T
        hot_hi = [half[:, hot_at + e * NB * T:hot_at + (e + 1) * NB * T].rearrange("p (j t) -> p j t", t=T)
                  for e in range(2)]
        split_i = shared[:, EP + EPAD:2 * EP + EPAD].bitcast(I32)
        same = shared[:, 0:T * P].bitcast(BF16).rearrange("p (b t e) -> p b t e", b=2, e=P)
        at = T * P
        pairs = []
        for _ in range(5):
            pairs.append(shared[:, at:at + T * 2 * D].rearrange("p (t s c) -> p t s c", t=T, s=2))
            at += T * 2 * D
        refl, xw, prod, mirrored, msgs = pairs
        dots = shared[:, at:at + 2 * T].rearrange("p (t s) -> p t s", s=2)
        scale2 = shared[:, at + 2 * T:at + 4 * T].rearrange("p (t s) -> p t s", s=2)
        late = shared[:, at + 4 * T:at + 5 * T]
        at += 5 * T
        PW = (0, R, R + D, R + 2 * D)
        msg_parts = shared[:, at:at + T * (PW[3] + 1) // 2].bitcast(BF16).rearrange("p (t c) -> p t c", t=T)
        assert at + T * (PW[3] + 1) // 2 <= WORDS and (PW[3] + 1) % 2 == 0
        acc_in = [shared[:, c * NB * D:(c + 1) * NB * D].rearrange("p (h c) -> p h c", c=D)
                  for c in range(COPIES)]
        node_xt = shared[:, COPIES * NB * D:COPIES * NB * D + NG * P]
        assert COPIES * NB * D + NG * P <= WORDS

        shared2 = sb("shared2", [P, max(2 * SLOTS * T * D, EP)])
        dst_i = shared2[:, 0:EP].bitcast(I32)
        sums = shared2[:, 0:SLOTS * T * D].rearrange("p (k t c) -> p k t c", k=SLOTS, t=T)
        merged = shared2[:, SLOTS * T * D:2 * SLOTS * T * D].rearrange("p (k t c) -> p k t c", k=SLOTS, t=T)

        idx = sb("idx", [P, SLOTS, T], I32)
        src_f = sb("src_f", [P, SLOTS, T])
        low_s = sb("low_s", [P, SLOTS, T], F16)
        high_s = sb("high_s", [P, SLOTS, T], F16)
        high_hot = sb("high_hot", [P, SLOTS, TP, NQ])
        keep_s = sb("keep_s", [P, SLOTS, T])
        put_i = sb("put_i", [P, SLOTS, T], I32)
        xsd = sb("xsd", [P, SLOTS, T, 2 * R])
        found = xsd[:, :, :, :].rearrange("p k t c -> p (k t c)")[:, 0:HB * BLOCK].rearrange("p (h b) -> p h b", b=BLOCK)
        first_tab = sb("first_tab", [P, R])
        xd_in = sb("xd_in", [P, SLOTS, T, R])
        rows = xd_in[:, :, :, :].rearrange("p k t c -> p (k t c)")[:, 0:SLOTS * T * D].rearrange(
            "p (k t c) -> p k t c", k=SLOTS, t=T)
        xt = sb("xt", [2 * D, BANK])
        hid = sb("hid", [P, BANK])
        lo_before, hi_same, hi_before = hid[:, 0:P], hid[:, P:P + NB], hid[:, P + NB:P + 2 * NB]

        node_x = sb("node_x", [P, NBP, D])
        node_tab = sb("node_tab", [P, NBP, R + 1])
        node_t = node_tab[:, :, :].rearrange("p h c -> p (h c)")[:, 0:NBP * D].rearrange("p (h c) -> p h c", c=D)
        agg = sb("agg", [P, NB, D])
        wide_tmp = sb("wide_tmp", [P, NBP * R])
        tmp = wide_tmp[:, 0:NB * D].rearrange("p (h c) -> p h c", c=D)
        cum = wide_tmp[:, 0:NB]
        node_h = sb("node_h", [P, NBP, D])
        cnt = sb("cnt", [P, 2, NB])
        start = sb("start", [P, NB + 1])
        probe_i = sb("probe_i", [P, NB], I32)
        start_i = sb("start_i", [P, NB], I32)
        end_i = sb("end_i", [P, NB], I32)
        has_in = sb("has_in", [P, NB])
        dinv = sb("dinv", [P, NB])
        dis = sb("dis", [P, NB])
        st = [sb(f"st{i}", [P, NB]) for i in range(4)]
        last_hi = sb("last_hi", [P, NB])
        last_lo = sb("last_lo", [P, P])
        last_row = sb("last_row", [P, D])

        ps = ctx.enter_context(nc.psum_tensor("ps", [P, 8 * BANK], F32))
        ps_xt = ps[0:2 * D, 0:BANK]
        ps_eq = ps[:, BANK:2 * BANK].rearrange("p (t e) -> p t e", e=P)
        ps_h = ps[:, 2 * BANK:3 * BANK]
        ps_mg = ps[:, 3 * BANK:3 * BANK + T * R].rearrange("p (t c) -> p t c", c=R)
        ps_v = ps[:, 4 * BANK:4 * BANK + T * 2 * D].rearrange("p (t c) -> p t c", c=2 * D)
        ps_low = ps[:, 3 * BANK:4 * BANK]
        ps_pair = [ps[:, (6 + b) * BANK:(7 + b) * BANK] for b in range(BANKS)]
        assert T * R <= BANK and T * 2 * D <= 2 * BANK and 2 * NQ * R <= BANK and QUAD * P == BANK
        ps_cnt = ps[:, 0:2 * NB]
        ps_dif = ps[:, BANK:BANK + NB]
        ps_firsts = ps[:, 2 * BANK:2 * BANK + NB]
        ps_next = ps[:, 3 * BANK:3 * BANK + NB]
        ps_span = ps[:, 0:NB * D]
        ps_nt = ps[:, 0:NG * P]
        ps_nh = ps[:, 4 * BANK:4 * BANK + NG * P]

        edges_cleared, edges_loaded = sem("edges_cleared"), sem("edges_loaded")
        weights_cleared, weights_loaded = sem("weights_cleared"), sem("weights_loaded")
        node_cleared, node_loaded = sem("node_cleared"), sem("node_loaded")
        zeros_ready, dram_cleared = sem("zeros_ready"), sem("dram_cleared")
        consts_ready, pool_made = sem("consts_ready"), sem("pool_made")
        hot_ready, hot_free, counted = sem("hot_ready"), sem("hot_free"), sem("counted")
        step_at_ready, steps_ready = sem("step_at_ready"), sem("steps_ready")
        cum_ready, differed = sem("cum_ready"), sem("differed")
        dst_blocked, blocks_stored = sem("dst_blocked"), sem("blocks_stored")
        firsts_ready, firsts_counted = sem("firsts_ready"), sem("firsts_counted")
        probe_ready, found_got = sem("probe_ready"), sem("found_got")
        start_ready, next_ready = sem("start_ready"), sem("next_ready")
        sqrt_in, sqrt_out = sem("sqrt_in"), sem("sqrt_out")
        table_ready = [sem(f"table_ready{l}") for l in range(3)]
        table_stored = [sem(f"table_stored{l}") for l in range(3)]
        starts_put, first_row = sem("starts_put"), sem("first_row")
        xd_loaded, xd_spread = sems("xd_loaded"), sem("xd_spread")
        idx_ready = [sem(f"idx_ready{l}") for l in range(3)]
        gathered = [sems(f"gathered{l}_") for l in range(3)]
        sums_ready = [sem(f"sums_ready{l}") for l in range(3)]
        sums_stored = [sems(f"sums_stored{l}_") for l in range(3)]
        span_in = [sem(f"span_in{l}") for l in range(3)]
        span_out = [sem(f"span_out{l}") for l in range(3)]
        ends_got = [sem(f"ends_got{l}") for l in range(3)]
        xt_ready, xt_copied, h_ready, h_done = sem("xt_ready"), sem("xt_copied"), sem("h_ready"), sem("h_done")
        row_ready, same_ready = sem("row_ready"), sem("same_ready")
        v_ready, v_free, msgs_ready = sem("v_ready"), sem("v_free"), sem("msgs_ready")
        parts_ready = [sem(f"parts_ready{l}") for l in range(3)]
        low_ready = [sem(f"low_ready{l}") for l in range(3)]
        low_copied = [sem(f"low_copied{l}") for l in range(3)]
        slot_hot = [sem(f"slot_hot{l}") for l in range(3)]
        pair_ready = [sem(f"pair_ready{l}") for l in range(3)]
        pair_free = [sem(f"pair_free{l}") for l in range(3)]
        picked = [sem(f"picked{l}") for l in range(3)]
        merge_ready, merged_ready = sem("merge_ready"), sem("merged_ready")
        scattered = sems("scattered")
        acc_loaded = sem("acc_loaded")
        pool_turn = sem("pool_turn")
        nt_in, nt_ready, nt_copied, nh_ready = sem("nt_in"), sem("nt_ready"), sem("nt_copied"), sem("nh_ready")
        tanh_in, tanh_out = sem("tanh_in"), sem("tanh_out")
        out_ready, out_stored = sem("out_ready"), sem("out_stored")
        dve_done = sem("dve_done")

        by_lo = "(h l) c -> l h c"
        src_v = src.rearrange("(p t) -> p t", p=P)
        dst_v = dst.rearrange("(p t) -> p t", p=P)
        xd_v = xd_rows.rearrange("(p t) c -> p t c", p=P)
        runsum_v = [r.rearrange("(p t) c -> p t c", p=P) for r in runsums]

        block = ctx.enter_context(nc.Block())

        @block.sync
        def _(sp):
            sp.wait_ge(edges_cleared, 1)
            sp.dma_start(src_i[:, 0:EP], src_v).then_inc(edges_loaded, 16)
            sp.dma_start(dst_i, dst_v).then_inc(edges_loaded, 16)
            sp.dma_start(prev_last[1:P, :], dst_v[0:P - 1, EP - 1:EP]).then_inc(edges_loaded, 16)
            sp.dma_start(next_first[0:P - 1, :], dst_v[1:P, 0:1]).then_inc(edges_loaded, 16)
            sp.wait_ge(node_cleared, 1)
            sp.dma_start(node_x[:, 0:NB - 1, :], x[0:(NB - 1) * P, :].rearrange(by_lo, l=P)).then_inc(node_loaded, 16)
            sp.dma_start(node_x[0:TAIL, NB - 1, :], x[(NB - 1) * P:N, :]).then_inc(node_loaded, 16)

            sp.wait_ge(dst_blocked, 1)
            sp.dma_start(dst_samples, picked_sb[:, 0:BLOCKS]).then_inc(blocks_stored, 16)
            sp.dma_start(dst_blocks.rearrange("(p b) c -> p (b c)", p=P), dst_f).then_inc(blocks_stored, 16)
            sp.wait_ge(zeros_ready, 1)
            for c in range(0, EP, CHUNK):
                sp.dma_start(xd_v[:, c:c + CHUNK, :], zeros.rearrange("p (t c) -> p t c", c=R)).then_inc(dram_cleared, 16)
            for c in range(COPIES):
                sp.dma_start(src_sums[c].rearrange("(p h) c -> p (h c)", p=P), zeros[:, 0:NB * D]).then_inc(dram_cleared, 16)

            sp.wait_ge(table_ready[0], 1)
            sp.dma_start(table0.rearrange(by_lo, l=P), node_tab[:, 0:NB, 0:R]).then_inc(table_stored[0], 16)
            sp.wait_ge(starts_put, 16 * NB)
            for k in range(SLOTS):
                sp.dma_start(xd_in[:, k], xd_v[:, k * T:(k + 1) * T, :]).then_inc(xd_loaded[k], 16)
                sp.sem_inc(sums_stored[0][k], 16)

            def load_rows(i, k):
                sp.wait_ge(xd_spread, i * SLOTS + (k + 1))
                sp.dma_start(xd_in[:, k], xd_v[:, bass.ds(i * STEP + (STEP + k * T), T), :]).then_inc(xd_loaded[k], 16)

            def store_sums(l, i, k):
                sp.wait_ge(sums_ready[l], i * SLOTS + (k + 1))
                sp.dma_start(runsum_v[l][:, bass.ds(i * STEP + k * T, T), :], sums[:, k]).then_inc(sums_stored[l][k], 16)

            with sp.Fori(0, ITERS - 1) as i:
                for k in range(SLOTS):
                    load_rows(i, k)
                    store_sums(0, i, k)
            load_rows(ITERS - 1, 0)
            for k in range(SLOTS):
                store_sums(0, ITERS - 1, k)
            store_sums(0, ITERS, 0)
            sp.wait_ge(merged_ready, GROUPS + 1)
            for b in range(SLOTS):
                sp.wait_ge(scattered[b], 16 * T * (ITERS + (b == 0)))
            for c in range(COPIES):
                sp.dma_start(acc_in[c], src_sums[c].rearrange(by_lo, l=P)).then_inc(acc_loaded, 16)

            for l in (1, 2):
                sp.wait_ge(table_ready[l], 1)
                sp.dma_start(tables[l - 1].rearrange(by_lo, l=P), node_t[:, 0:NB, :]).then_inc(table_stored[l], 16)
                for k in range(SLOTS):
                    sp.sem_inc(sums_stored[l][k], 16)
                with sp.Fori(0, ITERS) as i:
                    for k in range(SLOTS):
                        store_sums(l, i, k)
                store_sums(l, ITERS, 0)

            sp.wait_ge(out_ready, 1)
            sp.dma_start(out[0:(NB - 1) * P, :].rearrange(by_lo, l=P), agg[:, 0:NB - 1, :]).then_inc(out_stored, 16)
            sp.dma_start(out[(NB - 1) * P:N, :], agg[0:TAIL, NB - 1, :]).then_inc(out_stored, 16)
            sp.wait_ge(out_stored, 32)

        @block.gpsimd
        def _(pool):
            pool.memset(ident[:, :], 0.0).then_inc(pool_made, 1)
            for const in (follow, wrap, differ):
                pool.memset(const[:, :], 0.0).then_inc(pool_made, 1)
            pool.iota(iota_lo[:, :, :], pattern=[[1, P], [0, T]], base=0, channel_multiplier=0,
                      allow_small_or_imprecise_dtypes=True)
            pool.iota(iota_f[:, :], pattern=[[1, P]], base=0, channel_multiplier=0,
                      allow_small_or_imprecise_dtypes=True)
            pool.iota(slot_id[:, :], pattern=[[P, KT]], base=0, channel_multiplier=1,
                      allow_small_or_imprecise_dtypes=True)
            pool.iota(high_id[:, :], pattern=[[KT * P, NQ]], base=0, channel_multiplier=0,
                      allow_small_or_imprecise_dtypes=True)
            pool.iota(node_id[:, :], pattern=[[P, NB]], base=0, channel_multiplier=1,
                      allow_small_or_imprecise_dtypes=True)
            pool.iota(pow_i[:, :], pattern=[[0, 1]], base=127 + 63, channel_multiplier=-1)
            pool.wait_ge(pool_made, 4)
            for const, base in ((ident, 0), (follow, -1), (wrap, P - 1)):
                pool.affine_select(out=const[:, :], in_=const[:, :], compare_op=ALU.not_equal, fill=1.0,
                                   base=base, pattern=[[-1, P]], channel_multiplier=1)
            for n, (base, fill) in enumerate(((0, 1.0), (1, -1.0), (1 - P, 1.0))):
                pool.affine_select(out=differ[:, :], in_=differ[:, :], compare_op=ALU.not_equal, fill=fill,
                                   base=base, pattern=[[-1, P]], channel_multiplier=1).then_inc(pool_made, 1)
                pool.wait_ge(pool_made, 5 + n)
            pool.sem_inc(consts_ready, 1)

            def hold(semaphore, value):
                pool.wait_ge(semaphore, value)
                pool.sem_inc(pool_turn, 1)

            def gather(into, table, index):
                return pool.indirect_dma_start(out=into, out_offset=None, in_=table,
                                               in_offset=bass.IndirectOffsetOnAxis(index, 0))

            pool.wait_ge(blocks_stored, 32)
            for s in range(PROBES):
                pool.wait_ge(probe_ready, s + 1)
                for h in range(HB):
                    at = s % 2 * HB + h
                    gather(found[:, h, :], dst_samples if s < 2 else dst_blocks, probe_i[:, at:at + 1]).then_inc(found_got, 16)

            pool.wait_ge(table_stored[0], 16)
            pool.wait_ge(dram_cleared, 16 * (EP // CHUNK + COPIES))
            for h in range(NB):
                pool.indirect_dma_start(
                    out=xd_rows, out_offset=bass.IndirectOffsetOnAxis(start_i[:, h:h + 1], 0),
                    in_=node_tab[:, h, 1:R + 1], in_offset=None, bounds_check=E - 1, oob_is_err=False,
                ).then_inc(starts_put, 16)
            gather(first_tab[:, :], table0, first_i[:, :]).then_inc(first_row, 16)

            def gather_sources(k, j):
                for t in range(j * TD // BATCHES, (j + 1) * TD // BATCHES):
                    gather(xsd[:, k, t, 0:R], table0, idx[:, k, t:t + 1]).then_inc(gathered[0][k], 16)

            def scatter_messages(k, j):
                for t in range(j * BATCH, (j + 1) * BATCH):
                    pool.indirect_dma_start(
                        out=src_sums[t % COPIES], out_offset=bass.IndirectOffsetOnAxis(put_i[:, k, t:t + 1], 0),
                        in_=merged[:, k, t, :], in_offset=None, bounds_check=NPAD - 1, oob_is_err=False,
                        compute_op=ALU.add).then_inc(scattered[k], 16)

            LAG = SLOTS - 1

            def scatter_batch(i, b, j):
                if j == 0:
                    hold(merged_ready, i * SLOTS + (b + 2))
                    if b > 0:
                        hold(scattered[b - 1], i * (16 * T) + 16 * T)
                    elif not isinstance(i, int) or i > 0:
                        hold(scattered[SLOTS - 1], i * (16 * T))
                else:
                    hold(scattered[b], i * (16 * T) + 16 * BATCH * j)
                scatter_messages(b, j)

            for k in range(LAG):
                pool.wait_ge(idx_ready[0], k + 1)
                for j in range(BATCHES):
                    gather_sources(k, j)

            def gather_and_scatter(i, k, b_i, b):
                hold(idx_ready[0], i * SLOTS + (k + 1))
                for j in range(BATCHES):
                    gather_sources(k, j)
                    scatter_batch(b_i, b, j)

            gather_and_scatter(0, LAG, 0, 0)
            with pool.Fori(1, ITERS) as i:
                for k in range(LAG):
                    gather_and_scatter(i, k, i - 1, k + 1)
                gather_and_scatter(i, LAG, i, 0)
            gather_and_scatter(ITERS, 0, ITERS - 1, 1)
            for b_i, b in ((ITERS - 1, 2), (ITERS - 1, 3), (ITERS, 0)):
                for j in range(BATCHES):
                    scatter_batch(b_i, b, j)

            def gather_ends(l):
                for k in range(SLOTS):
                    pool.wait_ge(sums_stored[l][k], 16 * (ITERS + 1 + (k == 0)))
                for h in range(NB):
                    gather(agg[:, h, :], runsums[l], end_i[:, h:h + 1]).then_inc(ends_got[l], 16)

            gather_ends(0)
            for l in (1, 2):
                pool.wait_ge(table_stored[l], 16)

                def gather_rows(i, k):
                    hold(idx_ready[l], i * SLOTS + (k + 1))
                    for t in range(TD):
                        gather(rows[:, k, t, :], tables[l - 1], idx[:, k, t:t + 1]).then_inc(gathered[l][k], 16)

                with pool.Fori(0, ITERS) as i:
                    for k in range(SLOTS):
                        gather_rows(i, k)
                gather_rows(ITERS, 0)
                gather_ends(l)

        @block.scalar
        def _(act):
            act.wait_ge(weights_cleared, 1)
            w1_t = mlp_w1.rearrange("o f -> f o")
            w2_t = mlp_w2.rearrange("o f -> f o")
            n = 0
            for to, of in (
                (w1c[:, 0:HID], w1_t), (w1c[0:D, HID:P], w1_t[D:2 * D, :]), (w1c[D:2 * D, HID:P], w1_t[0:D, :]),
                (b1c[0:HID, :], mlp_b1.rearrange("(o a) -> o a", a=1)),
                (b1c[HID:P, :], mlp_b1.rearrange("(o a) -> o a", a=1)),
                (w2c[0:HID, 0:D], w2_t), (w2c[HID:P, D:2 * D], w2_t),
                (b2c[:, 0:D], mlp_b2.partition_broadcast(P)), (b2c[:, D:2 * D], mlp_b2.partition_broadcast(P)),
                (gcn_b[0][:, :], gcn_b1.partition_broadcast(P)), (gcn_b[1][:, :], gcn_b2.partition_broadcast(P)),
                *((gcn_w[l][b * D:(b + 1) * D, b * D:(b + 1) * D], w)
                  for l, w in enumerate((gcn_w1, gcn_w2)) for b in range(PER)),
            ):
                act.dma_start(to, of).then_inc(weights_loaded, 16)
                n += 1
            assert n == 11 + 2 * PER
            act.wait_ge(consts_ready, 1)

            def steps(g, e):
                act.wait_ge(step_at_ready, g + 1)
                for t in range(TS):
                    last = act.activation(step_lo[e][:, t, :], iota_f[:, :], ACT.Sign, bias=step_at[e][:, t:t + 1])
                last.then_inc(steps_ready, 1)

            with act.Fori(0, ITERS) as i:
                for k in range(SLOTS):
                    steps(i * SLOTS + k, k % 2)
            steps(GROUPS - 1, 0)

            def root(n):
                act.wait_ge(sqrt_in, n)
                act.activation(st[1][:, :], st[0][:, :], ACT.Sqrt).then_inc(sqrt_out, 1)

            root(1)
            root(2)
            act.wait_ge(weights_loaded, 16 * (11 + 2 * PER))

            def copy_low(l, n):
                act.wait_ge(low_ready[l], n)
                act.activation(low_row[:, :], ps_low, ACT.Copy).then_inc(low_copied[l], 1)

            def turn(g, second, first):
                for j, cols in enumerate(PARTS):
                    w = len(cols) * P
                    act.wait_ge(xt_ready, g * SUBS + (j + 1))
                    act.activation(xt[:, 0:w], ps_xt[:, 0:w], ACT.Copy).then_inc(xt_copied, 1)
                    if j == 1 and second:
                        copy_low(0, g * QUADS + 2 * QUADS)
                    if j == SUBS - 1 and first:
                        copy_low(0, g * QUADS + (2 * QUADS + 1))
                    act.wait_ge(h_ready, g * SUBS + (j + 1))
                    act.activation(hid[:, 0:w], ps_h[:, 0:w], ACT.Relu, bias=b1c[:, :]).then_inc(h_done, 1)

            for n in range(QUADS + 1):
                copy_low(0, n + 1)
            with act.Fori(0, GROUPS - 2) as g:
                turn(g, True, True)
            turn(GROUPS - 2, True, False)
            turn(GROUPS - 1, False, False)
            root(3)
            for l in (1, 2):
                act.wait_ge(nt_ready, l)
                for c in range(0, NG * P, BANK):
                    e = min(c + BANK, NG * P)
                    last = act.activation(node_xt[:, c:e], ps_nt[:, c:e], ACT.Copy)
                last.then_inc(nt_copied, 1)
                with act.Fori(0, GROUPS * QUADS + 1) as n:
                    copy_low(l, n + 1)
                act.wait_ge(tanh_in, l)
                act.activation(node_h[:, 0:NB, :], agg[:, :, :], ACT.Tanh).then_inc(tanh_out, 1)
            root(4)

        @block.tensor
        def _(pe):
            pe.wait_ge(firsts_ready, 1)
            nc.tensor.matmul(ps_firsts, lo_before, hi_same, start=True, stop=False)
            nc.tensor.matmul(ps_firsts, ones[:, :], hi_before, start=False, stop=True).then_inc(firsts_counted, 1)
            pe.wait_ge(zeros_ready, 1)
            nc.tensor.matmul(ps_cnt, zeros[:, 0:P], zeros[:, 0:2 * NB], start=True, stop=False)

            def count_group(g, e):
                pe.wait_ge(hot_ready, g + 1)
                for t in range(TH):
                    nc.tensor.matmul(ps_cnt[:, 0:NB], hot_lo[e][:, :, t], hot_hi[e][:, :, t], start=False, stop=False)
                pe.wait_ge(steps_ready, g + 1)
                for t in range(TS):
                    last = nc.tensor.matmul(ps_cnt[:, NB:2 * NB], step_lo[e][:, t, :], hot_hi[e][:, :, TH + t],
                                            start=False, stop=False)
                last.then_inc(hot_free, 1)

            with pe.Fori(0, GROUPS // 2) as i:
                for e in range(2):
                    count_group(i * 2 + e, e)
            count_group(GROUPS - 1, 0)
            nc.tensor.matmul(ps_cnt, zeros[:, 0:P], zeros[:, 0:2 * NB], start=False, stop=True).then_inc(counted, 1)
            pe.wait_ge(consts_ready, 1)
            pe.wait_ge(start_ready, 1)
            nc.tensor.matmul(ps_next, follow[:, :], start[:, 0:NB], start=True, stop=False)
            nc.tensor.matmul(ps_next, wrap[:, :], start[:, 1:NB + 1], start=False, stop=True).then_inc(next_ready, 1)
            pe.wait_ge(cum_ready, 1)
            nc.tensor.matmul(ps_dif, differ[:, :], cum, start=True, stop=True).then_inc(differed, 1)

            pe.wait_ge(weights_loaded, 16 * (11 + 2 * PER))

            def spread_low(l, k, q):
                for u in range(QUAD):
                    t = TD + q * QUAD + u
                    last = nc.tensor.matmul(ps_low[:, u * P:(u + 1) * P], low_s[:, k, t:t + 1].to_broadcast([P, P]),
                                            ident_h[:, :], start=True, stop=True)
                last.then_inc(low_ready[l], 1)

            def gather_column(l, w, u, bank):
                q, c0, at = u // QUAD, u % QUAD * P, u % 2 * NQ * w
                for c in range(KT):
                    for part in range(3):
                        last = nc.tensor.matmul(ps_pair[bank][:, at:at + NQ * w], hot[:, q, c, c0:c0 + P],
                                                parts[:, c, part, 0:NQ * w],
                                                start=c == part == 0, stop=c == KT - 1 and part == 2)
                if u % 2:
                    last.then_inc(pair_ready[l], 1)

            def count(i, k, per, more):
                return i * (SLOTS * per) + (k * per + more)

            def merge(i, k):
                pe.wait_ge(msgs_ready, count(i, k, 1, 1))
                for t in range(T):
                    for part in range(3):
                        w = R if part == 0 else D
                        last = nc.tensor.matmul(ps_mg[:, t, 0:w], same[:, k % 2, t, :], msg_parts[:, t, PW[part]:PW[part] + w],
                                                start=part == 0, stop=part == 2)
                last.then_inc(merge_ready, 1)

            def turn(i, k, merges=True, nexts=2):
                s = k % SLOTS
                columns = {0: (0,), 1: (1,), 2: (2,), 3: (3,), 4: (4, 5), 5: (6,), 6: (7,)}
                pe.wait_ge(gathered[0][s], (i + k // SLOTS) * (16 * TD) + 16 * TD)
                pe.wait_ge(picked[0], count(i, k, PAIRS, PAIRS))
                pe.wait_ge(xd_spread, count(i, k, 1, 1))
                def reflections(j):
                    pe.wait_ge(h_done, count(i, k, SUBS, j + 1))
                    if j == 0:
                        pe.wait_ge(v_free, count(i, k, 1, 1))
                    for u, t in enumerate(PARTS[j]):
                        last = nc.tensor.matmul(ps_v[:, t, :], hid[:, u * P:(u + 1) * P], w2c[:, :], start=True, stop=True)
                    if j == SUBS - 1:
                        last.then_inc(v_ready, 1)

                for j, cols in enumerate(PARTS):
                    for u, t in enumerate(cols):
                        last = nc.tensor.transpose(ps_xt[:, u * P:(u + 1) * P], xsd[:, s, t, 1:1 + 2 * D], ident[:, :])
                    last.then_inc(xt_ready, 1)
                    if nexts > 0:
                        for u in columns[j]:
                            if u % QUAD == 0:
                                pe.wait_ge(slot_hot[0], count(i, k, QUADS, QUADS + u // QUAD + 1))
                            if u % 2 == 0:
                                pe.wait_ge(pair_free[0], count(i, k, PAIRS, PAIRS + u // 2 + 1))
                            gather_column(0, R, u, u // 2 % BANKS)
                        if j == 1:
                            if merges:
                                pe.wait_ge(merged_ready, count(i, k, 1, 0))
                            spread_low(0, (k + 1) % SLOTS, 1)
                    if j == SUBS - 1 and nexts > 1:
                        pe.wait_ge(idx_ready[0], count(i, k, 1, 3))
                        spread_low(0, (k + 2) % SLOTS, 0)
                    if j > 0:
                        reflections(j - 1)
                        pe.wait_ge(same_ready, count(i, k, SUBS, j))
                    for u, t in enumerate(cols):
                        for add, of in enumerate((low_s, high_s)):
                            last = nc.tensor.matmul(ps_eq[:, u, :], of[:, s, t:t + 1].to_broadcast([P, P]), ident_h[:, :],
                                                    start=add == 0, stop=add == 1)
                    last.then_inc(row_ready, 1)
                    pe.wait_ge(xt_copied, count(i, k, SUBS, j + 1))
                    w = len(cols) * P
                    nc.tensor.matmul(ps_h[:, 0:w], w1c[:, :], xt[:, 0:w], start=True, stop=True).then_inc(h_ready, 1)
                reflections(SUBS - 1)
                pe.wait_ge(same_ready, count(i, k, SUBS, SUBS))
                if merges:
                    if nexts > 1:
                        pe.wait_ge(low_copied[0], count(i, k, QUADS, 2 * QUADS + 1))
                    else:
                        pe.wait_ge(low_copied[0], GROUPS * QUADS)
                    merge(i, k - 1)

            pe.wait_ge(parts_ready[0], 1)
            pe.wait_ge(idx_ready[0], SLOTS)
            spread_low(0, 0, 0)
            for u in range(TP):
                if u % QUAD == 0:
                    pe.wait_ge(slot_hot[0], u // QUAD + 1)
                    if u == 0:
                        spread_low(0, 0, 1)
                    else:
                        spread_low(0, 1, 0)
                if u % 2 == 0:
                    pe.wait_ge(pair_free[0], u // 2 + 1)
                gather_column(0, R, u, u // 2 % BANKS)
            turn(0, 0, merges=False)
            with pe.Fori(0, ITERS - 1) as i:
                for k in range(1, SLOTS + 1):
                    turn(i, k)
            for g in range((ITERS - 1) * SLOTS + 1, GROUPS):
                turn(ITERS - 1, g - (ITERS - 1) * SLOTS, nexts=GROUPS - 1 - g)
            merge(ITERS, 0)

            def spans(l):
                pe.wait_ge(span_in[l], 1)
                flat = tmp[:, :, :].rearrange("p h c -> p (h c)")
                for c in range(0, NB * D, BANK):
                    e = min(c + BANK, NB * D)
                    last = nc.tensor.matmul(ps_span[:, c:e], last_lo[:, :], flat[:, c:e], start=True, stop=True)
                last.then_inc(span_out[l], 1)

            spans(0)
            for l in (1, 2):
                pe.wait_ge(nt_in, l)
                flat = node_h[:, :, :].rearrange("p h c -> p (h c)")
                for b in range(NG):
                    last = nc.tensor.transpose(ps_nt[:, b * P:(b + 1) * P], flat[:, b * P:(b + 1) * P], ident[:, :])
                last.then_inc(nt_ready, 1)
                pe.wait_ge(nt_copied, l)
                for b in range(NG):
                    last = nc.tensor.matmul(ps_nh[:, b * P:(b + 1) * P], node_xt[:, b * P:(b + 1) * P], gcn_w[l - 1][:, :],
                                            start=True, stop=True)
                last.then_inc(nh_ready, 1)

                def gather_group(i, k):
                    for q in range(QUADS):
                        pe.wait_ge(slot_hot[l], count(i, k, QUADS, q + 1))
                        if q == QUADS - 1:
                            pe.wait_ge(idx_ready[l], count(i, k, 1, 2))
                            spread_low(l, (k + 1) % SLOTS, 0)
                        else:
                            spread_low(l, k, q + 1)
                        for u in range(q * QUAD, (q + 1) * QUAD):
                            if u % 2 == 0:
                                pe.wait_ge(pair_free[l], count(i, k, PAIRS, u // 2 + 1))
                            gather_column(l, D, u, u // 2 % BANKS)

                pe.wait_ge(parts_ready[l], 1)
                pe.wait_ge(idx_ready[l], SLOTS)
                spread_low(l, 0, 0)
                with pe.Fori(0, ITERS) as i:
                    for k in range(SLOTS):
                        gather_group(i, k)
                gather_group(ITERS, 0)
                pe.wait_ge(low_copied[l], GROUPS * QUADS + 1)
                spans(l)

        @block.vector
        def _(dve):
            v = nc.vector
            done = [0]
            base = [0]

            def step(ins):
                done[0] += 1
                ins.then_inc(dve_done, 1)
                dve.wait_ge(dve_done, base[0] + done[0])

            v.memset(prev_last[:, :], -1)
            v.memset(src_i[:, EP:], 0)
            v.memset(keep[:, EP:], 0.0)
            v.memset(low_h[:, EP:], 0.0)
            v.memset(high_h[:, EP:], 0.0)
            v.memset(next_first[:, :], -1).then_inc(edges_cleared, 1)
            v.memset(gcn_w[0][:, :], 0.0)
            v.memset(gcn_w[1][:, :], 0.0)
            v.memset(w2c[:, :], 0.0).then_inc(weights_cleared, 1)
            v.memset(node_x[:, :, :], 0.0).then_inc(node_cleared, 1)
            v.memset(zeros, 0.0).then_inc(zeros_ready, 1)
            v.memset(ones[:, :], 1.0)
            v.memset(node_tab[:, :, :], 0.0)
            step(v.memset(node_h[:, :, :], 0.0))
            dve.wait_ge(consts_ready, 1)
            v.tensor_copy(ident_h[:, :], ident[:, :])
            step(v.tensor_scalar(pow2_i[:, :], pow_i[:, :], 23, None, ALU.logical_shift_left))
            step(v.tensor_scalar(lead_max[:, :], pow2, 2.0, None, ALU.mult))

            dve.wait_ge(edges_loaded, 16 * 4)
            v.memset(dst_f[:, EP:], float(FAR))
            step(v.tensor_copy(dst_f[:, 0:EP], dst_i))
            v.tensor_copy(picked_sb[:, 0:BLOCKS], dst_f.rearrange("p (b c) -> p b c", c=BLOCK)[:, :, 0]).then_inc(dst_blocked, 1)
            v.tensor_scalar(first_lohi_i[:, 0:1], dst_i[:, 0:1], P - 1, None, ALU.bitwise_and)
            step(v.tensor_scalar(first_lohi_i[:, 1:2], dst_i[:, 0:1], P.bit_length() - 1, None, ALU.arith_shift_right))
            step(v.tensor_copy(first_lohi[:, :], first_lohi_i[:, :]))
            v.tensor_scalar(lo_before, iota_f[:, :], first_lohi[:, 0:1], None, ALU.is_gt)
            v.tensor_scalar(hi_same, iota_f[:, 0:NB], first_lohi[:, 1:2], None, ALU.is_equal)
            v.tensor_scalar(hi_before, iota_f[:, 0:NB], first_lohi[:, 1:2], None, ALU.is_gt).then_inc(firsts_ready, 1)
            step(v.tensor_scalar(split_i, src_i[:, 0:EP], P - 1, None, ALU.bitwise_and))
            step(v.tensor_copy(src_lohi[0], split_i))
            step(v.tensor_scalar(split_i, src_i[:, 0:EP], P.bit_length() - 1, None, ALU.arith_shift_right))
            step(v.tensor_copy(src_lohi[1], split_i))
            v.tensor_tensor(keep[:, 1:EP], dst_i[:, 1:EP], dst_i[:, 0:EP - 1], ALU.is_equal)
            v.tensor_tensor(keep[:, 0:1], dst_i[:, 0:1], prev_last[:, :], ALU.is_equal)
            v.tensor_tensor(runs_on[:, :], dst_i[:, EP - 1:EP], next_first[:, :], ALU.is_equal)
            v.tensor_copy(first_i[:, :], dst_i[:, 0:1])
            v.tensor_scalar(last_lohi_i[:, 0:1], dst_i[:, EP - 1:EP], P - 1, None, ALU.bitwise_and)
            step(v.tensor_scalar(last_lohi_i[:, 1:2], dst_i[:, EP - 1:EP], P.bit_length() - 1, None, ALU.arith_shift_right))
            step(v.tensor_copy(last_lohi[:, :], last_lohi_i[:, :]))
            v.tensor_scalar(last_lo[:, :], iota_f[:, :], last_lohi[:, 0:1], None, ALU.is_equal)
            step(v.tensor_scalar(last_hi[:, :], iota_f[:, 0:NB], last_lohi[:, 1:2], None, ALU.is_equal))

            def one_hots(e, col):
                v.tensor_scalar(step_at[e][:, :], src_lohi[0][:, bass.ds(col + TH, TS)], -1.0, 0.5, ALU.mult,
                                ALU.add).then_inc(step_at_ready, 1)
                lo = src_lohi[0][:, bass.ds(col, TH)].unsqueeze(1)
                hi = src_lohi[1][:, bass.ds(col, T)].unsqueeze(1)
                v.tensor_tensor(hot_lo[e], lo.to_broadcast([P, P, TH]), iota_lo[:, :, 0:TH], ALU.is_equal)
                v.tensor_tensor(hot_hi[e], hi.to_broadcast([P, NB, T]), iota_lo[:, 0:NB, :], ALU.is_equal).then_inc(hot_ready, 1)

            part, block, hits, row = st
            dve.wait_ge(firsts_counted, 1)
            step(v.tensor_scalar(part[:, :], ps_firsts, -1.0, 0.0, ALU.add, ALU.max))
            v.tensor_copy(probe_i[:, :], part[:, :]).then_inc(probe_ready, 1)

            def probe(s):
                cols = slice(s % 2 * HB, (s % 2 + 1) * HB)
                dve.wait_ge(found_got, 16 * HB * (s + 1))
                step(v.tensor_tensor(found, found, node_id[:, cols].unsqueeze(2).to_broadcast([P, HB, BLOCK]), ALU.is_lt))
                step(v.tensor_reduce(hits[:, cols], found, AX.X, ALU.add))
                if s < 2:
                    step(v.tensor_scalar(block[:, cols], hits[:, cols], -1.0, 0.0, ALU.add, ALU.max))
                    step(v.tensor_scalar(row[:, cols], part[:, cols], float(BLOCKS), None, ALU.mult))
                    step(v.tensor_tensor(row[:, cols], row[:, cols], block[:, cols], ALU.add))
                    v.tensor_copy(probe_i[:, cols], row[:, cols]).then_inc(probe_ready, 1)
                else:
                    step(v.tensor_scalar(part[:, cols], part[:, cols], float(EP), None, ALU.mult))
                    step(v.tensor_scalar(block[:, cols], block[:, cols], float(BLOCK), None, ALU.mult))
                    step(v.tensor_tensor(part[:, cols], part[:, cols], block[:, cols], ALU.add))
                    last = v.tensor_tensor(start[:, cols], part[:, cols], hits[:, cols], ALU.add)
                    if s == PROBES - 1:
                        last.then_inc(start_ready, 1)
                    else:
                        last.then_inc(probe_ready, 1)

            v.memset(start[:, NB:NB + 1], float(E))
            for e in range(2):
                one_hots(e, e * T)
            pairs_of = [1 + s * (GROUPS // 2 - 1) // (PROBES + 1) for s in range(PROBES + 2)]
            for s in range(PROBES + 1):
                with dve.Fori(pairs_of[s], pairs_of[s + 1]) as i:
                    for e in range(2):
                        dve.wait_ge(hot_free, i * 2 + (e - 1))
                        one_hots(e, i * (2 * T) + e * T)
                if s < PROBES:
                    probe(s)
            dve.wait_ge(hot_free, GROUPS - 2)
            one_hots(0, (GROUPS - 1) * T)
            dve.wait_ge(next_ready, 1)
            step(v.tensor_tensor(cnt[:, 1, :], ps_next, start[:, 0:NB], ALU.subtract))
            dve.wait_ge(counted, 1)
            v.tensor_copy(cnt[:, 0, :], ps_cnt[:, 0:NB])
            v.tensor_copy(cum, ps_cnt[:, NB:2 * NB]).then_inc(cum_ready, 1)
            dve.wait_ge(differed, 1)
            step(v.tensor_scalar(cum, ps_dif, 0.5, None, ALU.mult))
            step(v.tensor_tensor(cnt[:, 0, :], cnt[:, 0, :], cum, ALU.add))

            def rsqrt(n, to, arg):
                dve.wait_ge(sqrt_out, n)
                step(v.reciprocal(st[2][:, :], st[1][:, :]))
                step(v.tensor_tensor(st[3][:, :], st[2][:, :], st[2][:, :], ALU.mult))
                step(v.tensor_tensor(st[3][:, :], st[3][:, :], arg, ALU.mult))
                step(v.tensor_scalar(st[3][:, :], st[3][:, :], -0.5, 1.5, ALU.mult, ALU.add))
                step(v.tensor_tensor(to, st[2][:, :], st[3][:, :], ALU.mult))

            step(v.tensor_tensor(st[0][:, :], cnt[:, 0, :], cnt[:, 1, :], ALU.add))
            v.tensor_scalar(st[0][:, :], st[0][:, :], DEG_MIN, None, ALU.max).then_inc(sqrt_in, 1)
            dve.wait_ge(sqrt_in, 1)
            rsqrt(1, dis[:, :], st[0][:, :])
            v.tensor_scalar(st[0][:, :], cnt[:, 1, :], 1.0, None, ALU.add).then_inc(sqrt_in, 1)
            dve.wait_ge(sqrt_in, 2)
            rsqrt(2, dinv[:, :], st[0][:, :])
            step(v.tensor_scalar(has_in[:, :], cnt[:, 1, :], 0.0, None, ALU.is_gt))
            step(v.tensor_tensor(st[0][:, :], start[:, 0:NB], cnt[:, 1, :], ALU.add))
            step(v.tensor_scalar(end_i[:, :], st[0][:, :], -1.0, 0.0, ALU.add, ALU.max))
            step(v.tensor_scalar(st[1][:, :], has_in[:, :], -float(FAR), float(FAR), ALU.mult, ALU.add))
            step(v.tensor_tensor(start_i[:, :], st[1][:, :], start[:, 0:NB], ALU.add))
            dve.wait_ge(node_loaded, 32)
            v.tensor_copy(node_tab[:, 0:NB, 1:R], node_x[:, 0:NB, :])
            v.tensor_copy(node_tab[:, 0:NB, R:R + 1], dis[:, :].unsqueeze(2))
            v.tensor_copy(node_tab[:, 0:NB, 0:1], dis[:, :].unsqueeze(2)).then_inc(table_ready[0], 1)
            step(v.tensor_scalar(split_i, src_i[:, 0:EP], KT * P - 1, None, ALU.bitwise_and))
            step(v.tensor_copy(low_h[:, 0:EP], split_i))
            step(v.tensor_tensor(high_h[:, 0:EP], src_i[:, 0:EP], split_i, ALU.subtract))

            def split_table(l, table, w):
                rest = wide_tmp[:, 0:NBP * w].rearrange("p (h c) -> p h c", c=w)
                by = "p (b k) c -> p k b c"
                left = table
                for part in range(3):
                    piece = parts[:, :, part, 0:NQ * w].rearrange("p k (b c) -> p k b c", c=w)
                    if part < 2:
                        step(v.tensor_copy(piece, left.rearrange(by, k=KT)))
                        step(v.tensor_tensor(rest.rearrange(by, k=KT), left.rearrange(by, k=KT), piece, ALU.subtract))
                        left = rest
                    else:
                        v.tensor_copy(piece, left.rearrange(by, k=KT)).then_inc(parts_ready[l], 1)
                dve.wait_ge(parts_ready[l], 1)

            def stage(l, k, col):
                if l == 0:
                    v.tensor_copy(src_f[:, k, :], src_i[:, bass.ds(col, T)])
                v.tensor_copy(keep_s[:, k, :], keep[:, bass.ds(col, T)])
                v.tensor_copy(low_s[:, k, :], low_h[:, bass.ds(col, T)])
                step(v.tensor_copy(high_s[:, k, :], high_h[:, bass.ds(col, T)]))
                v.tensor_tensor(high_hot[:, k, :, :], high_s[:, k, TD:].unsqueeze(2).to_broadcast([P, TP, NQ]),
                                high_id[:, :].unsqueeze(1).to_broadcast([P, TP, NQ]), ALU.is_equal)
                v.tensor_copy(idx[:, k, :], src_i[:, bass.ds(col, T)]).then_inc(idx_ready[l], 1)

            def count(i, k, per, more):
                return i * (SLOTS * per) + (k * per + more)

            def hot_rows(l, i, k, q):
                dve.wait_ge(low_copied[l], count(i, k, QUADS, q + 1))
                for c in range(KT):
                    last = v.tensor_scalar(hot[:, q, c, :], low_row[:, :], slot_id[:, c:c + 1], None, ALU.is_equal)
                last.then_inc(slot_hot[l], 1)

            def pick(l, w, i, k, pair, bank, to):
                s = k % SLOTS
                prods = picked_sb[:, 0:2 * NQ * w].rearrange("p (t b c) -> p t b c", t=2, c=w)
                dve.wait_ge(pair_ready[l], count(i, k, PAIRS, pair + 1))
                v.tensor_tensor(prods, ps_pair[bank][:, 0:2 * NQ * w].rearrange("p (t b c) -> p t b c", t=2, c=w),
                                high_hot[:, s, 2 * pair:2 * pair + 2, :].unsqueeze(3).to_broadcast([P, 2, NQ, w]),
                                ALU.mult).then_inc(pair_free[l], 1)
                dve.wait_ge(pair_free[l], count(i, k, PAIRS, pair + 1 + BANKS))
                v.tensor_reduce(to, prods.rearrange("p t b c -> p t c b"), AX.X, ALU.add).then_inc(picked[l], 1)
                dve.wait_ge(picked[l], count(i, k, PAIRS, pair + 1))

            def running_sums(l, i, k, values):
                s = k % SLOTS
                dve.wait_ge(sums_stored[l][s], (i + k // SLOTS) * 16 + 16)
                for c in range(D):
                    last = v.tensor_tensor_scan(sums[:, s, :, c], keep_s[:, s, :], values(c),
                                                sums[:, (s - 1) % SLOTS, T - 1, c:c + 1], ALU.mult, ALU.add)
                last.then_inc(sums_ready[l], 1)
                dve.wait_ge(sums_ready[l], count(i, k, 1, 1))

            def start_pass(l):
                step(v.memset(sums[:, SLOTS - 1, T - 1, :], 0.0))
                for k in range(SLOTS):
                    stage(l, k, k * T)
                dve.wait_ge(idx_ready[l], SLOTS)
                dve.sem_inc(pair_free[l], BANKS)

            split_table(0, node_tab[:, :, 0:R], R)
            step(v.tensor_copy(msg_parts[:, :, D], pow2.to_broadcast([P, T])))
            dve.sem_inc(v_free, 1)
            dve.sem_inc(merged_ready, 1)
            start_pass(0)
            dve.wait_ge(weights_loaded, 16 * (11 + 2 * PER))

            def spread_rows(i, k):
                s = k % SLOTS
                dve.wait_ge(xd_loaded[s], (i + k // SLOTS) * 16 + 16)
                for c in range(R):
                    last = v.tensor_tensor_scan(xsd[:, s, :, R + c], keep_s[:, s, :], xd_in[:, s, :, c],
                                                xsd[:, (s - 1) % SLOTS, T - 1, R + c:R + c + 1], ALU.mult, ALU.add)
                last.then_inc(xd_spread, 1)
                dve.wait_ge(xd_spread, count(i, k, 1, 1))

            def equal_sources(i, k, j):
                s, part = k % SLOTS, PARTS[j]
                cols, w = slice(part.start, part.stop), len(part)
                dve.wait_ge(row_ready, count(i, k, SUBS, j + 1))
                v.tensor_tensor(same[:, k % 2, cols, :], ps_eq[:, 0:w, :],
                                src_f[:, s, cols].unsqueeze(2).to_broadcast([P, w, P]), ALU.is_equal).then_inc(same_ready, 1)

            def pick_rows(i, k, pair):
                t = TD + 2 * pair
                pick(0, R, i, k, pair, pair % BANKS, xsd[:, k % SLOTS, t:t + 2, 0:R])

            def turn(i, k, nexts=3):
                g1 = count(i, k, 1, 1)
                wide = [P, T, 2, D]

                def equal(j):
                    if nexts > 0:
                        equal_sources(i, k + 1, j)

                def hot(q):
                    if nexts > 1:
                        hot_rows(0, i, k + 2, q)

                def pick(pair):
                    if nexts > 1:
                        pick_rows(i, k + 2, pair)

                dve.wait_ge(v_ready, g1)
                v.tensor_tensor(refl.rearrange("p t s c -> p t (s c)"), ps_v,
                                b2c[:, :].unsqueeze(1).to_broadcast([P, T, 2 * D]), ALU.add).then_inc(v_free, 1)
                dve.wait_ge(v_free, count(i, k, 1, 2))
                step(v.tensor_tensor(prod, refl, refl, ALU.mult))
                equal(0)
                if nexts > 1:
                    spread_rows(i, k + 2)
                step(v.tensor_reduce(scale2, prod, AX.X, ALU.add))
                step(v.tensor_scalar(scale2, scale2, NORM_MIN, 0.5, ALU.max, ALU.mult))
                equal(1)
                step(v.reciprocal(scale2, scale2))
                step(v.tensor_tensor(xw, xsd[:, k % SLOTS, :, 1:1 + 2 * D].rearrange("p t (s c) -> p t s c", s=2),
                                     xsd[:, k % SLOTS, :, 0:2 * R:2 * R - 1].unsqueeze(3).to_broadcast(wide), ALU.mult))
                equal(2)
                pick(0)
                hot(1)
                step(v.tensor_tensor(prod, refl, xw, ALU.mult))
                step(v.tensor_reduce(dots, prod, AX.X, ALU.add))
                step(v.tensor_tensor(dots, dots, scale2, ALU.mult))
                step(v.tensor_tensor(prod, refl, dots.unsqueeze(3).to_broadcast(wide), ALU.mult))
                equal(3)
                step(v.tensor_tensor(mirrored, xw, prod, ALU.subtract))
                pick(1)
                for s in range(2):
                    last = v.tensor_tensor(prod[:, :, s, :], refl[:, :, s, :], mirrored[:, :, 1 - s, :], ALU.mult)
                step(last)
                equal(4)
                step(v.tensor_reduce(dots, prod, AX.X, ALU.add))
                step(v.tensor_tensor(dots, dots, scale2, ALU.mult))
                step(v.tensor_tensor(prod, refl, dots.unsqueeze(3).to_broadcast(wide), ALU.mult))
                equal(5)
                for s in range(2):
                    last = v.tensor_tensor(msgs[:, :, s, :], mirrored[:, :, 1 - s, :], prod[:, :, s, :], ALU.subtract)
                step(last)
                left = msgs[:, :, 0, :]
                for part in range(3):
                    piece = msg_parts[:, :, PW[part]:PW[part] + D]
                    if part < 2:
                        step(v.tensor_copy(piece, left))
                        step(v.tensor_tensor(prod[:, :, 0, :], left, piece, ALU.subtract))
                        left = prod[:, :, 0, :]
                    else:
                        v.tensor_copy(piece, left).then_inc(msgs_ready, 1)
                pick(2)
                running_sums(0, i, k, lambda c: msgs[:, :, 1, c])
                equal(6)
                pick(3)
                if nexts > 2:
                    hot_rows(0, i, k + 3, 0)
                dve.wait_ge(merge_ready, g1)
                step(v.tensor_scalar(late, ps_mg[:, :, D], lead_max[:, :], float(SKIP), ALU.is_gt, ALU.mult))
                step(v.tensor_tensor(put_i[:, k % SLOTS, :], late, src_f[:, k % SLOTS, :], ALU.add))
                v.tensor_copy(merged[:, k % SLOTS, :, :], ps_mg[:, :, 0:D]).then_inc(merged_ready, 1)
                stage(0, k % SLOTS, i * STEP + (STEP + k * T))

            dve.wait_ge(dram_cleared, 16 * (EP // CHUNK + COPIES))
            for q in range(QUADS):
                hot_rows(0, 0, 0, q)
                pick_rows(0, 0, 2 * q)
                pick_rows(0, 0, 2 * q + 1)
            hot_rows(0, 0, 1, 0)
            dve.wait_ge(first_row, 16)
            v.tensor_copy(xsd[:, SLOTS - 1, T - 1, R:R + D], first_tab[:, 1:R])
            step(v.tensor_copy(xsd[:, SLOTS - 1, T - 1, R + D:2 * R], first_tab[:, 0:1]))
            spread_rows(0, 0)
            spread_rows(0, 1)
            for j in range(SUBS):
                equal_sources(0, 0, j)
                if j in (1, 3, 4, 6):
                    pick_rows(0, 1, (1, 3, 4, 6).index(j))
                if j == 2:
                    hot_rows(0, 0, 1, 1)
            hot_rows(0, 0, 2, 0)
            LINKS = 22
            before_loop = done[0]
            with dve.Fori(0, ITERS - 1) as i:
                done[0], base[0] = 0, i * (LINKS * SLOTS) + before_loop
                for k in range(SLOTS):
                    turn(i, k)
                assert done[0] == LINKS * SLOTS, done[0]
            base[0], done[0] = 0, before_loop + (ITERS - 1) * LINKS * SLOTS
            for g in range((ITERS - 1) * SLOTS, GROUPS):
                turn(ITERS - 1, g - (ITERS - 1) * SLOTS, nexts=GROUPS - 1 - g)

            def node_sums(l):
                step(v.tensor_scalar(last_row[:, :], sums[:, (GROUPS - 1) % SLOTS, T - 1, :], runs_on[:, :], None, ALU.mult))
                v.tensor_tensor(tmp[:, :, :], last_hi[:, :].unsqueeze(2).to_broadcast([P, NB, D]),
                                last_row[:, :].unsqueeze(1).to_broadcast([P, NB, D]), ALU.mult).then_inc(span_in[l], 1)
                dve.wait_ge(ends_got[l], 16 * NB)
                step(v.tensor_tensor(agg[:, :, :], agg[:, :, :], has_in[:, :].unsqueeze(2).to_broadcast([P, NB, D]), ALU.mult))
                dve.wait_ge(span_out[l], 1)
                step(v.tensor_tensor(agg[:, :, :], agg[:, :, :], ps_span.rearrange("p (h c) -> p h c", c=D), ALU.add))

            def per_node(a):
                return a[:, :].unsqueeze(2).to_broadcast([P, NB, D])

            def layernorm(n, to, a):
                step(v.tensor_reduce(st[0][:, :], a, AX.X, ALU.add))
                step(v.tensor_scalar(st[0][:, :], st[0][:, :], 1.0 / D, None, ALU.mult))
                step(v.tensor_tensor(a, a, per_node(st[0]), ALU.subtract))
                step(v.tensor_tensor(tmp[:, :, :], a, a, ALU.mult))
                step(v.tensor_reduce(st[0][:, :], tmp[:, :, :], AX.X, ALU.add))
                v.tensor_scalar(st[0][:, :], st[0][:, :], 1.0 / D, LN_EPS, ALU.mult, ALU.add).then_inc(sqrt_in, 1)
                dve.wait_ge(sqrt_in, n)
                rsqrt(n, st[3][:, :], st[0][:, :])
                return v.tensor_tensor(to, a, per_node(st[3]), ALU.mult)

            node_sums(0)
            dve.wait_ge(acc_loaded, 16 * COPIES)
            for c in range(COPIES):
                step(v.tensor_tensor(agg[:, :, :], agg[:, :, :], acc_in[c], ALU.add))
            step(v.tensor_tensor(agg[:, :, :], agg[:, :, :], per_node(dis), ALU.mult))
            step(v.tensor_tensor(agg[:, :, :], agg[:, :, :], node_x[:, 0:NB, :], ALU.add))
            step(v.tensor_scalar(agg[:, :, :], agg[:, :, :], 0.0, None, ALU.max))
            step(v.tensor_tensor(agg[:, :, :], agg[:, :, :], node_x[:, 0:NB, :], ALU.add))
            step(layernorm(3, node_h[:, 0:NB, :], agg[:, :, :]))
            v.tensor_copy(node_x[:, 0:NB, :], node_h[:, 0:NB, :]).then_inc(nt_in, 1)

            for l in (1, 2):
                dve.wait_ge(nh_ready, l)
                step(v.tensor_tensor(node_t[:, 0:NB, :], ps_nh[:, 0:NB * D].rearrange("p (h c) -> p h c", c=D),
                                     per_node(dinv), ALU.mult))
                v.memset(node_t[:, NB:, :], 0.0).then_inc(table_ready[l], 1)
                dve.wait_ge(table_ready[l], 1)
                split_table(l, node_t, D)
                for k in range(SLOTS):
                    dve.wait_ge(sums_stored[l - 1][k], 16 * (ITERS + 1 + (k == 0)))
                start_pass(l)

                def turn(i, k):
                    to = rows[:, k, TD:, :]
                    pick(l, D, i, k, 0, 0, to[:, 0:2, :])
                    hot_rows(l, i, k, 1)
                    pick(l, D, i, k, 1, 1, to[:, 2:4, :])
                    pick(l, D, i, k, 2, 0, to[:, 4:6, :])
                    hot_rows(l, i, k + 1, 0)
                    pick(l, D, i, k, 3, 1, to[:, 6:8, :])
                    dve.wait_ge(gathered[l][k], i * (16 * TD) + 16 * TD)
                    running_sums(l, i, k, lambda c: rows[:, k, :, c])
                    stage(l, k, i * STEP + (STEP + k * T))

                hot_rows(l, 0, 0, 0)
                before_loop = done[0]
                with dve.Fori(0, ITERS) as i:
                    done[0], base[0] = 0, i * SLOTS + before_loop
                    for k in range(SLOTS):
                        turn(i, k)
                    assert done[0] == SLOTS
                base[0], done[0] = 0, before_loop + ITERS * SLOTS
                turn(ITERS, 0)
                node_sums(l)
                step(v.tensor_tensor(agg[:, :, :], agg[:, :, :], node_t[:, 0:NB, :], ALU.add))
                step(v.tensor_tensor(agg[:, :, :], agg[:, :, :], per_node(dinv), ALU.mult))
                v.tensor_tensor(agg[:, :, :], agg[:, :, :], gcn_b[l - 1][:, :].unsqueeze(1).to_broadcast([P, NB, D]),
                                ALU.add).then_inc(tanh_in, 1)
                dve.wait_ge(tanh_out, l)
                if l == 1:
                    dve.drain().then_inc(nt_in, 1)
            step(v.tensor_tensor(node_x[:, 0:NB, :], node_x[:, 0:NB, :], node_h[:, 0:NB, :], ALU.add))
            layernorm(4, agg[:, :, :], node_x[:, 0:NB, :]).then_inc(out_ready, 1)


_INS = ['x', 'src', 'dst', 'L0_gnn_W1', 'L0_gnn_b1', 'L0_gnn_W2', 'L0_gnn_b2',
        'L1_gnn_W1', 'L1_gnn_b1', 'L1_gnn_W2', 'L1_gnn_b2']


def kernel(**inputs):
    import numpy as _np
    import concourse.bacc as _bacc
    from concourse import mybir as _mybir
    from concourse.bass_utils import run_bass_kernel_spmd as _run

    nc = _bacc.Bacc("TRN2", target_bir_lowering=False, num_devices=1)
    arrays, args = {}, []
    for name in _INS:
        a = _np.ascontiguousarray(inputs[name])
        arrays[f"in_{name}_dram"] = a
        args.append(nc.dram_tensor(f"in_{name}_dram", a.shape, _mybir.dt.from_np(a.dtype), kind="ExternalInput").ap())
    args.append(nc.dram_tensor("out_0_dram", inputs["x"].shape, _mybir.dt.float32, kind="ExternalOutput").ap())
    gnn_kernel(nc, *args)
    r = _run(nc, [arrays], core_ids=[0])
    return r.results[0]["out_0_dram"]
```
